# Optimizing a Trainium2 kernel written in Bass

```python
import numpy as np
import jax
import jax.numpy as jnp

def _softmax(x, axis=-1):
    return jax.nn.softmax(x, axis=axis)

def _gelu(x):
    return jax.nn.gelu(x, approximate=True)

def _silu(x):
    return jax.nn.silu(x)

def _sigmoid(x):
    return jax.nn.sigmoid(x)

def _layernorm(x, axis=-1, eps=1e-05):
    m = jnp.mean(x, axis=axis, keepdims=True)
    v = jnp.var(x, axis=axis, keepdims=True)
    return (x - m) / jnp.sqrt(v + eps)

def _scatter_add(tgt, idx, src, axis=0):
    return tgt.at[idx].add(src)

def _segment_sum(src, seg, n):
    return jax.ops.segment_sum(src, seg, n)
kernel_name = 'mk_adaln_attn_ffn_d1_seqx_r8_ce7639'

def setup_inputs(seed: int=0):
    np.random.seed(seed)
    _w = jnp.asarray

    def _rec_inputs():
        import jax
        import jax.numpy as jnp
        _rk = jax.random.key(seed)
        x = -0.0003929 + 0.9999 * jax.random.normal(jax.random.fold_in(_rk, 1), (32, 32, 512), jnp.float32)
        _lenS = 32 - jax.random.randint(jax.random.fold_in(_rk, 7), (32,), 0, max(1, 32 // 4) + 1, jnp.int32)
        _lenS2 = 32 - jax.random.randint(jax.random.fold_in(_rk, 8), (32,), 0, max(1, 32 // 4) + 1, jnp.int32)
        cond_512 = 0.00782532 + 1.00527 * jax.random.normal(jax.random.fold_in(_rk, 11), (32, 64), jnp.float32)
        return (x, cond_512)
    x, cond_512 = _rec_inputs()

    def _L0_cond_setup():
        import jax, jax.numpy as jnp
        from jax import lax
        import numpy as np
        CIN, COUT, K, STYLE_DIM = (32, 32, 3, 64)
        N_LAYERS = 4
        TYPES = ('same', 'upsample', 'same', 'downsample')
        SCALE = 1.0 / float(np.sqrt(CIN * K ** 2))
        EPS = 1e-08
        _BK = np.array([1.0, 3.0, 3.0, 1.0], dtype=np.float32)
        BLUR_K = _BK / _BK.sum()

        def _blur(x, kern, pad):
            B, C, _ = x.shape
            xp = jnp.pad(x, ((0, 0), (0, 0), (pad[0], pad[1])))
            w = jnp.broadcast_to(kern.astype(x.dtype)[None, None, :], (C, 1, kern.shape[0]))
            return lax.conv_general_dilated(xp, w, (1,), 'VALID', feature_group_count=C, dimension_numbers=('NCH', 'OIH', 'NCH'))

        def _conv_same(x, w):
            p = (K - 1) // 2
            return lax.conv_general_dilated(x[None], w, (1,), [(p, p)], dimension_numbers=('NCH', 'OIH', 'NCH'))[0]

        def _conv_down(x, w):
            return lax.conv_general_dilated(x[None], w, (2,), 'VALID', dimension_numbers=('NCH', 'OIH', 'NCH'))[0]

        def _conv_up(x, w_t):
            return lax.conv_transpose(x[None], w_t, (2,), 'VALID', dimension_numbers=('NCH', 'IOH', 'NCH'), transpose_kernel=True)[0]

        def _layer(x, style, w, b, mw, mb, typ):
            s = style @ mw.T + mb
            weight = SCALE * w * s[:, None, :, None]
            demod = lax.rsqrt(jnp.sum(weight * weight, axis=(2, 3)) + EPS)
            weight = weight * demod[:, :, None, None]
            blur_k = jnp.asarray(BLUR_K)
            if typ == 'same':
                out = jax.vmap(_conv_same)(x, weight) + b[None, :, None]
            elif typ == 'upsample':
                out = jax.vmap(_conv_up)(x, weight.transpose(0, 2, 1, 3)) + b[None, :, None]
                out = _blur(out, 2.0 * blur_k, (1, 1))
            elif typ == 'downsample':
                xb = _blur(x, blur_k, (2, 2))
                out = jax.vmap(_conv_down)(xb, weight) + b[None, :, None]
            else:
                raise NotImplementedError(typ)
            return out
        key = jax.random.key(seed)
        ks = jax.random.split(key, 6)
        B, L = (16, 512)
        return {'x': jax.random.normal(ks[0], (B, CIN, L), dtype=jnp.float32), 'style': jax.random.normal(ks[1], (B, STYLE_DIM), dtype=jnp.float32), 'weights': jax.random.normal(ks[2], (N_LAYERS, COUT, CIN, K), dtype=jnp.float32), 'biases': jax.random.normal(ks[3], (N_LAYERS, COUT), dtype=jnp.float32) * 0.1, 'mod_w': jax.random.normal(ks[4], (N_LAYERS, CIN, STYLE_DIM), dtype=jnp.float32) / np.sqrt(STYLE_DIM), 'mod_b': 1.0 + 0.1 * jax.random.normal(ks[5], (N_LAYERS, CIN), dtype=jnp.float32)}
    _L0_cond_all = _L0_cond_setup()
    _L0_cond_in = {k: v for k, v in _L0_cond_all.items() if k in ('weights', 'biases', 'mod_w', 'mod_b')}
    del _L0_cond_all

    def _L0_attn_setup():
        import math
        import jax, jax.numpy as jnp
        import numpy as np
        N_HEADS = 32
        ALIBI_BIAS_MAX = 8

        def _alibi_slopes(n_heads, alibi_bias_max=8):
            _n = 2 ** math.ceil(math.log2(n_heads))
            m = jnp.arange(1, _n + 1, dtype=jnp.float32) * (alibi_bias_max / _n)
            slopes = 1.0 / jnp.power(2.0, m)
            if _n != n_heads:
                slopes = jnp.concatenate([slopes[1::2], slopes[::2]])[:n_heads]
            return slopes
        key = jax.random.key(seed)
        k1, k2, k3 = jax.random.split(key, 3)
        B, S, D = (1, 256, 512)
        x = jax.random.normal(k1, (B, S, D), dtype=jnp.float32)
        w_qkv = jax.random.normal(k2, (3 * D, D), dtype=jnp.float32) * 0.02
        b_qkv = jnp.zeros((3 * D,), dtype=jnp.float32)
        w_out = jax.random.normal(k3, (D, D), dtype=jnp.float32) * 0.02
        b_out = jnp.zeros((D,), dtype=jnp.float32)
        return {'x': x, 'w_qkv': w_qkv, 'b_qkv': b_qkv, 'w_out': w_out, 'b_out': b_out}
    _L0_attn_all = _L0_attn_setup()
    _L0_attn_in = {k: v for k, v in _L0_attn_all.items() if k in ('w_qkv', 'b_qkv', 'w_out', 'b_out')}
    del _L0_attn_all

    def _L0_cond2_setup():
        import jax, jax.numpy as jnp
        from jax import lax
        import numpy as np
        CIN, COUT, K, STYLE_DIM = (32, 32, 3, 64)
        N_LAYERS = 4
        TYPES = ('same', 'upsample', 'same', 'downsample')
        SCALE = 1.0 / float(np.sqrt(CIN * K ** 2))
        EPS = 1e-08
        _BK = np.array([1.0, 3.0, 3.0, 1.0], dtype=np.float32)
        BLUR_K = _BK / _BK.sum()

        def _blur(x, kern, pad):
            B, C, _ = x.shape
            xp = jnp.pad(x, ((0, 0), (0, 0), (pad[0], pad[1])))
            w = jnp.broadcast_to(kern.astype(x.dtype)[None, None, :], (C, 1, kern.shape[0]))
            return lax.conv_general_dilated(xp, w, (1,), 'VALID', feature_group_count=C, dimension_numbers=('NCH', 'OIH', 'NCH'))

        def _conv_same(x, w):
            p = (K - 1) // 2
            return lax.conv_general_dilated(x[None], w, (1,), [(p, p)], dimension_numbers=('NCH', 'OIH', 'NCH'))[0]

        def _conv_down(x, w):
            return lax.conv_general_dilated(x[None], w, (2,), 'VALID', dimension_numbers=('NCH', 'OIH', 'NCH'))[0]

        def _conv_up(x, w_t):
            return lax.conv_transpose(x[None], w_t, (2,), 'VALID', dimension_numbers=('NCH', 'IOH', 'NCH'), transpose_kernel=True)[0]

        def _layer(x, style, w, b, mw, mb, typ):
            s = style @ mw.T + mb
            weight = SCALE * w * s[:, None, :, None]
            demod = lax.rsqrt(jnp.sum(weight * weight, axis=(2, 3)) + EPS)
            weight = weight * demod[:, :, None, None]
            blur_k = jnp.asarray(BLUR_K)
            if typ == 'same':
                out = jax.vmap(_conv_same)(x, weight) + b[None, :, None]
            elif typ == 'upsample':
                out = jax.vmap(_conv_up)(x, weight.transpose(0, 2, 1, 3)) + b[None, :, None]
                out = _blur(out, 2.0 * blur_k, (1, 1))
            elif typ == 'downsample':
                xb = _blur(x, blur_k, (2, 2))
                out = jax.vmap(_conv_down)(xb, weight) + b[None, :, None]
            else:
                raise NotImplementedError(typ)
            return out
        key = jax.random.key(seed)
        ks = jax.random.split(key, 6)
        B, L = (16, 512)
        return {'x': jax.random.normal(ks[0], (B, CIN, L), dtype=jnp.float32), 'style': jax.random.normal(ks[1], (B, STYLE_DIM), dtype=jnp.float32), 'weights': jax.random.normal(ks[2], (N_LAYERS, COUT, CIN, K), dtype=jnp.float32), 'biases': jax.random.normal(ks[3], (N_LAYERS, COUT), dtype=jnp.float32) * 0.1, 'mod_w': jax.random.normal(ks[4], (N_LAYERS, CIN, STYLE_DIM), dtype=jnp.float32) / np.sqrt(STYLE_DIM), 'mod_b': 1.0 + 0.1 * jax.random.normal(ks[5], (N_LAYERS, CIN), dtype=jnp.float32)}
    _L0_cond2_all = _L0_cond2_setup()
    _L0_cond2_in = {k: v for k, v in _L0_cond2_all.items() if k in ('weights', 'biases', 'mod_w', 'mod_b')}
    del _L0_cond2_all

    def _L0_ffn_setup():
        import jax, jax.numpy as jnp
        import numpy as np
        B, T, D_IN, D_OUT = (8, 256, 512, 512)
        N_LORAS, RANK = (16, 32)
        SCALING = 1.0
        key = jax.random.key(seed)
        ks = jax.random.split(key, 8)
        std = 1.0 / D_IN ** 0.5
        x = jax.random.normal(ks[0], (B, T, D_IN), dtype=jnp.float32)
        idx = jax.random.randint(ks[1], (B,), 0, N_LORAS)
        gate = jax.nn.one_hot(idx, N_LORAS, dtype=jnp.float32)
        kernel = jax.random.normal(ks[2], (D_IN, D_OUT), dtype=jnp.float32) * std
        bias = jnp.zeros((D_OUT,), dtype=jnp.float32)
        lora_A = jax.random.normal(ks[3], (N_LORAS, RANK, D_IN), dtype=jnp.float32) * std
        lora_B = jax.random.normal(ks[4], (N_LORAS, D_OUT, RANK), dtype=jnp.float32) * 0.01
        lora_A_shared = jax.random.normal(ks[5], (RANK, D_IN), dtype=jnp.float32) * std
        lora_B_shared = jax.random.normal(ks[6], (D_OUT, RANK), dtype=jnp.float32) * 0.01
        return {'x': x, 'gate': gate, 'kernel': kernel, 'bias': bias, 'lora_A': lora_A, 'lora_B': lora_B, 'lora_A_shared': lora_A_shared, 'lora_B_shared': lora_B_shared}
    _L0_ffn_all = _L0_ffn_setup()
    _L0_ffn_in = {k: v for k, v in _L0_ffn_all.items() if k in ('gate', 'kernel', 'bias', 'lora_A', 'lora_B', 'lora_A_shared', 'lora_B_shared')}
    del _L0_ffn_all
    return {'x': x, 'cond_512': cond_512, 'L0_cond_weights': _L0_cond_in['weights'], 'L0_cond_biases': _L0_cond_in['biases'], 'L0_cond_mod_w': _L0_cond_in['mod_w'], 'L0_cond_mod_b': _L0_cond_in['mod_b'], 'L0_attn_w_qkv': _L0_attn_in['w_qkv'], 'L0_attn_b_qkv': _L0_attn_in['b_qkv'], 'L0_attn_w_out': _L0_attn_in['w_out'], 'L0_attn_b_out': _L0_attn_in['b_out'], 'L0_cond2_weights': _L0_cond2_in['weights'], 'L0_cond2_biases': _L0_cond2_in['biases'], 'L0_cond2_mod_w': _L0_cond2_in['mod_w'], 'L0_cond2_mod_b': _L0_cond2_in['mod_b'], 'L0_ffn_gate': _L0_ffn_in['gate'], 'L0_ffn_kernel': _L0_ffn_in['kernel'], 'L0_ffn_bias': _L0_ffn_in['bias'], 'L0_ffn_lora_A': _L0_ffn_in['lora_A'], 'L0_ffn_lora_B': _L0_ffn_in['lora_B'], 'L0_ffn_lora_A_shared': _L0_ffn_in['lora_A_shared'], 'L0_ffn_lora_B_shared': _L0_ffn_in['lora_B_shared']}

def reference(x, cond_512, L0_cond_weights, L0_cond_biases, L0_cond_mod_w, L0_cond_mod_b, L0_attn_w_qkv, L0_attn_b_qkv, L0_attn_w_out, L0_attn_b_out, L0_cond2_weights, L0_cond2_biases, L0_cond2_mod_w, L0_cond2_mod_b, L0_ffn_gate, L0_ffn_kernel, L0_ffn_bias, L0_ffn_lora_A, L0_ffn_lora_B, L0_ffn_lora_A_shared, L0_ffn_lora_B_shared):
    import jax
    import jax.numpy as jnp

    def _L0_cond_ref(x, style, weights, biases, mod_w, mod_b):
        import jax, jax.numpy as jnp
        from jax import lax
        import numpy as np
        CIN, COUT, K, STYLE_DIM = (32, 32, 3, 64)
        N_LAYERS = 4
        TYPES = ('same', 'upsample', 'same', 'downsample')
        SCALE = 1.0 / float(np.sqrt(CIN * K ** 2))
        EPS = 1e-08
        _BK = np.array([1.0, 3.0, 3.0, 1.0], dtype=np.float32)
        BLUR_K = _BK / _BK.sum()

        def _blur(x, kern, pad):
            B, C, _ = x.shape
            xp = jnp.pad(x, ((0, 0), (0, 0), (pad[0], pad[1])))
            w = jnp.broadcast_to(kern.astype(x.dtype)[None, None, :], (C, 1, kern.shape[0]))
            return lax.conv_general_dilated(xp, w, (1,), 'VALID', feature_group_count=C, dimension_numbers=('NCH', 'OIH', 'NCH'))

        def _conv_same(x, w):
            p = (K - 1) // 2
            return lax.conv_general_dilated(x[None], w, (1,), [(p, p)], dimension_numbers=('NCH', 'OIH', 'NCH'))[0]

        def _conv_down(x, w):
            return lax.conv_general_dilated(x[None], w, (2,), 'VALID', dimension_numbers=('NCH', 'OIH', 'NCH'))[0]

        def _conv_up(x, w_t):
            return lax.conv_transpose(x[None], w_t, (2,), 'VALID', dimension_numbers=('NCH', 'IOH', 'NCH'), transpose_kernel=True)[0]

        def _layer(x, style, w, b, mw, mb, typ):
            s = style @ mw.T + mb
            weight = SCALE * w * s[:, None, :, None]
            demod = lax.rsqrt(jnp.sum(weight * weight, axis=(2, 3)) + EPS)
            weight = weight * demod[:, :, None, None]
            blur_k = jnp.asarray(BLUR_K)
            if typ == 'same':
                out = jax.vmap(_conv_same)(x, weight) + b[None, :, None]
            elif typ == 'upsample':
                out = jax.vmap(_conv_up)(x, weight.transpose(0, 2, 1, 3)) + b[None, :, None]
                out = _blur(out, 2.0 * blur_k, (1, 1))
            elif typ == 'downsample':
                xb = _blur(x, blur_k, (2, 2))
                out = jax.vmap(_conv_down)(xb, weight) + b[None, :, None]
            else:
                raise NotImplementedError(typ)
            return out
        out = x
        for i, typ in enumerate(TYPES):
            out = _layer(out, style, weights[i], biases[i], mod_w[i], mod_b[i], typ)
        return out

    def _L0_attn_ref(x, w_qkv, b_qkv, w_out, b_out):
        import math
        import jax, jax.numpy as jnp
        import numpy as np
        N_HEADS = 32
        ALIBI_BIAS_MAX = 8

        def _alibi_slopes(n_heads, alibi_bias_max=8):
            _n = 2 ** math.ceil(math.log2(n_heads))
            m = jnp.arange(1, _n + 1, dtype=jnp.float32) * (alibi_bias_max / _n)
            slopes = 1.0 / jnp.power(2.0, m)
            if _n != n_heads:
                slopes = jnp.concatenate([slopes[1::2], slopes[::2]])[:n_heads]
            return slopes
        B, S, D = x.shape
        H = N_HEADS
        hd = D // H
        qkv = jnp.einsum('bsd,od->bso', x, w_qkv) + b_qkv
        q, k, v = jnp.split(qkv, 3, axis=-1)
        q = q.reshape(B, S, H, hd)
        k = k.reshape(B, S, H, hd)
        v = v.reshape(B, S, H, hd)
        scale = 1.0 / math.sqrt(hd)
        scores = jnp.einsum('bqhd,bkhd->bhqk', q, k) * scale
        slopes = _alibi_slopes(H, ALIBI_BIAS_MAX)
        positions = jnp.arange(1 - S, 1, dtype=jnp.float32)
        alibi = slopes[:, None] * positions[None, :]
        scores = scores + alibi[None, :, None, :]
        causal = jnp.arange(S)[:, None] >= jnp.arange(S)[None, :]
        scores = jnp.where(causal[None, None, :, :], scores, jnp.float32(-1000000000.0))
        attn = jax.nn.softmax(scores, axis=-1)
        out = jnp.einsum('bhqk,bkhd->bqhd', attn, v).reshape(B, S, D)
        return jnp.einsum('bsd,od->bso', out, w_out) + b_out

    def _L0_cond2_ref(x, style, weights, biases, mod_w, mod_b):
        import jax, jax.numpy as jnp
        from jax import lax
        import numpy as np
        CIN, COUT, K, STYLE_DIM = (32, 32, 3, 64)
        N_LAYERS = 4
        TYPES = ('same', 'upsample', 'same', 'downsample')
        SCALE = 1.0 / float(np.sqrt(CIN * K ** 2))
        EPS = 1e-08
        _BK = np.array([1.0, 3.0, 3.0, 1.0], dtype=np.float32)
        BLUR_K = _BK / _BK.sum()

        def _blur(x, kern, pad):
            B, C, _ = x.shape
            xp = jnp.pad(x, ((0, 0), (0, 0), (pad[0], pad[1])))
            w = jnp.broadcast_to(kern.astype(x.dtype)[None, None, :], (C, 1, kern.shape[0]))
            return lax.conv_general_dilated(xp, w, (1,), 'VALID', feature_group_count=C, dimension_numbers=('NCH', 'OIH', 'NCH'))

        def _conv_same(x, w):
            p = (K - 1) // 2
            return lax.conv_general_dilated(x[None], w, (1,), [(p, p)], dimension_numbers=('NCH', 'OIH', 'NCH'))[0]

        def _conv_down(x, w):
            return lax.conv_general_dilated(x[None], w, (2,), 'VALID', dimension_numbers=('NCH', 'OIH', 'NCH'))[0]

        def _conv_up(x, w_t):
            return lax.conv_transpose(x[None], w_t, (2,), 'VALID', dimension_numbers=('NCH', 'IOH', 'NCH'), transpose_kernel=True)[0]

        def _layer(x, style, w, b, mw, mb, typ):
            s = style @ mw.T + mb
            weight = SCALE * w * s[:, None, :, None]
            demod = lax.rsqrt(jnp.sum(weight * weight, axis=(2, 3)) + EPS)
            weight = weight * demod[:, :, None, None]
            blur_k = jnp.asarray(BLUR_K)
            if typ == 'same':
                out = jax.vmap(_conv_same)(x, weight) + b[None, :, None]
            elif typ == 'upsample':
                out = jax.vmap(_conv_up)(x, weight.transpose(0, 2, 1, 3)) + b[None, :, None]
                out = _blur(out, 2.0 * blur_k, (1, 1))
            elif typ == 'downsample':
                xb = _blur(x, blur_k, (2, 2))
                out = jax.vmap(_conv_down)(xb, weight) + b[None, :, None]
            else:
                raise NotImplementedError(typ)
            return out
        out = x
        for i, typ in enumerate(TYPES):
            out = _layer(out, style, weights[i], biases[i], mod_w[i], mod_b[i], typ)
        return out

    def _L0_ffn_ref(x, gate, kernel, bias, lora_A, lora_B, lora_A_shared, lora_B_shared):
        import jax, jax.numpy as jnp
        import numpy as np
        B, T, D_IN, D_OUT = (8, 256, 512, 512)
        N_LORAS, RANK = (16, 32)
        SCALING = 1.0
        base_out = jnp.matmul(x, kernel) + bias
        b = gate.shape[0]
        x_flat = x.reshape(b, -1, x.shape[-1])
        A_eff = jnp.einsum('bn,nri->bri', gate, lora_A)
        B_eff = jnp.einsum('bn,nor->bor', gate, lora_B)
        Ax = jnp.einsum('bri,bti->btr', A_eff, x_flat)
        delta_flat = jnp.einsum('bor,btr->bto', B_eff, Ax)
        Ax_s = jnp.einsum('ri,bti->btr', lora_A_shared, x_flat)
        delta_flat = delta_flat + jnp.einsum('or,btr->bto', lora_B_shared, Ax_s)
        delta = delta_flat.reshape(x.shape[:-1] + (kernel.shape[-1],))
        return base_out + (SCALING * delta).astype(base_out.dtype)
    x = x + _L0_attn_ref(_L0_cond_ref(x, cond_512, L0_cond_weights, L0_cond_biases, L0_cond_mod_w, L0_cond_mod_b), L0_attn_w_qkv, L0_attn_b_qkv, L0_attn_w_out, L0_attn_b_out)
    x = x + _L0_ffn_ref(_L0_cond2_ref(x, cond_512, L0_cond2_weights, L0_cond2_biases, L0_cond2_mod_w, L0_cond2_mod_b), L0_ffn_gate, L0_ffn_kernel, L0_ffn_bias, L0_ffn_lora_A, L0_ffn_lora_B, L0_ffn_lora_A_shared, L0_ffn_lora_B_shared)
    return x

_drawn_inputs = setup_inputs


def setup_inputs(seed=0):
    import zlib

    import numpy as np

    out = dict(_drawn_inputs(seed))
    spreads = {'L0_attn_b_qkv': (0.0, 0.1), 'L0_attn_b_out': (0.0, 0.1), 'L0_ffn_bias': (0.0, 0.1)}
    factors = {}
    for name, (base, spread) in spreads.items():
        noise = np.random.default_rng([zlib.crc32(name.encode()), seed]).standard_normal(out[name].shape)
        drawn = base * np.exp(spread * noise) if base else spread * noise
        out[name] = jnp.asarray(drawn.astype(out[name].dtype))
    for name, factor in factors.items():
        out[name] = (out[name] * factor).astype(out[name].dtype)
    return out
```

```python
from contextlib import ExitStack

import numpy as np

import concourse.bass as bass
from concourse import mybir

F32 = mybir.dt.float32
ALU = mybir.AluOpType
ACT = mybir.ActivationFunctionType
AX_X = mybir.AxisListType.X

B, C, L = 32, 32, 512
STYLE = 64
TAPS, PH = 3, 4
M = L // PH
MP = M + 2
G, GB = 8, 4
HG = G // 2
NL = 4
HEADS, HD = 32, 16
NT = L // 128
NQKV = 3 * NT
LORAS, RANK = 16, 32
BANKS = 8
SCALE = 1.0 / float(np.sqrt(C * TAPS ** 2))
EPS = 1e-8
BLUR = [0.125, 0.375, 0.375, 0.125]
BLUR_EDGE = 0.125
QK_SCALE = 1.0 / float(np.sqrt(HD))

C_ID, C_ALIBI, C_MASK = 0, 128, 128 + HEADS * C
C_SEL = C_MASK + 4
N_CONST = C_SEL + C


def shape_constants():
    out = np.zeros((128, N_CONST), np.float32)
    out[:, C_ID:C_ID + 128] = np.eye(128)
    slopes = (1.0 / 2.0 ** (np.arange(1, HEADS + 1, dtype=np.float32) * np.float32(8.0 / HEADS))).astype(np.float32)
    k, q = np.arange(C), np.arange(128) % C
    for r2 in range(2):
        for t in range(NT):
            for c in range(4):
                at = C_ALIBI + ((r2 * NT + t) * 4 + c) * C
                bias = slopes[8 * t + 4 * r2 + c] * (k - (C - 1)).astype(np.float32)
                out[:, at:at + C] = np.where(q[:, None] >= k[None, :], bias[None, :], np.float32(-1e9))
    for c in range(4):
        out[:, C_MASK + c] = (np.arange(128) % 64) // HD == c
    out[:, C_SEL:C_SEL + C] = np.tile(np.eye(C), (4, 1))
    return out


def build(nc, x, style, cw, cb, cmw, cmb, w_qkv, b_qkv, w_out, b_out, gate, ffn_w, ffn_b,
          lora_a, lora_b, lora_as, lora_bs, consts, out):
    ctx = ExitStack()
    with ctx:
        def sb(name, shape):
            return ctx.enter_context(nc.sbuf_tensor(name, shape, F32))

        def sem(name):
            return ctx.enter_context(nc.semaphore(name))

        acc = ctx.enter_context(nc.psum_tensor("acc", [128, BANKS, 512], F32))
        const = sb("const", [128, N_CONST])
        ident = const[:, C_ID:C_ID + 128]
        xres = sb("xres", [128, G, L])
        xs = sb("xs", [128, 2, PH, M])
        xp = sb("xp", [128, HG, GB, MP])
        z1 = xp
        z2 = sb("z2", [128, 2, 2, GB, MP])
        z3 = sb("z3", [128, 2, 2, GB, MP])
        halo = sb("halo", [128, 2, GB, M])
        cT = sb("cT", [128, HG, PH, 128])
        qT = sb("qT", [128, 2, NT, 128])
        kT = sb("kT", [128, 2, NT, 128])
        km = sb("km", [128, 2, 2, 4, 128])
        v2 = sb("v2", [128, HG, 2, L])
        S = sb("S", [128, HG, HEADS * C])
        pblk = sb("pblk", [128, 2, 16, 128])
        stat = sb("stat", [128, 2, HG, HEADS])
        oT = sb("oT", [128, 2, NT * 128])
        wqkvT = sb("wqkvT", [128, PH, NQKV * 128])
        woT = sb("woT", [128, NT, L])
        bqk = sb("bqk", [128, 2 * NT])
        rows = sb("rows", [128, 3, L])
        bv_row, bo_row, bf_row = rows[:, 0, :], rows[:, 1, :], rows[:, 2, :]
        aT = sb("aT", [128, PH, G + 1, RANK])
        bT4 = sb("bT4", [128, 2, L])
        bT = sb("bT", [64, 2, L])
        axT = sb("axT", [64, 2, 128])

        wnat = sb("wnat", [128, C * TAPS])
        w2rep = sb("w2rep", [128, C * TAPS])
        mwnat = sb("mwnat", [128, STYLE])
        styn = sb("styn", [32, STYLE])
        styT = sb("styT", [STYLE, B])
        wT = sb("wT", [128, 2, TAPS, NL, C])
        mbr = sb("mbr", [128, 2, NL])
        cbr = sb("cbr", [128, 2, NL])
        b4row = sb("b4row", [128, 2, C])
        stab = sb("stab", [128, NL, B])
        taps2 = sb("taps2", [128, 2, 6, C])
        taps4 = sb("taps4", [128, 2, 6, C])
        t1 = sb("t1", [128, 2, PH, C])
        t2 = sb("t2", [128, 2, 2, PH, C])
        t3 = sb("t3", [128, 2, PH, C])
        t4 = sb("t4", [128, 2, 3, PH, C])
        sin = sb("sin", [128, 2, G])
        tabA = sb("tabA", [128, 2, 3, B])
        tabB = sb("tabB", [128, 2, 3, B])
        edge = sb("edge", [128, 2, B])
        scale32 = sb("scale32", [32, 128])
        d4row = sb("d4row", [128, 2, B, C])
        gsm = sb("gsm", [128, NT, G])

        wq_nat = S[:, :, :].rearrange("p a b -> p (a b)")[:, 0:4096].rearrange("p (t l) -> p t l", t=8)
        wv_nat = pblk[:, :, :, :].rearrange("p a b c -> p (a b c)")[:, 0:2048].rearrange("p (t l) -> p t l", t=4)
        wo_nat = pblk[:, :, :, :].rearrange("p a b c -> p (a b c)")[:, 2048:4096].rearrange("p (t l) -> p t l", t=4)
        v2f = v2[:, :, :, :].rearrange("p a b c -> p (a b c)")
        la_nat = v2f[:, 0:2048].rearrange("p (t l) -> p t l", t=4)
        lb_nat = v2f[:, 2048:4096].rearrange("p (t n r) -> p t n r", t=4, r=RANK)
        kmf = km[:, :, :, :, :].rearrange("p a b c d -> p (a b c d)")
        lbT = kmf.rearrange("p (t l) -> p t l", t=4)
        gmat = qT[:, :, :, :].rearrange("p a b c -> p (a b c)").rearrange("p (t g r) -> p t g r", t=4, g=G)
        kTf = kT[:, :, :, :].rearrange("p a b c -> p (a b c)")
        las_nat = kTf[0:32, 0:512]
        lbs_nat = kTf[:, 512:640].rearrange("p (t r) -> p t r", t=4)

        oTf = oT[:, :, :].rearrange("p a b -> p (a b)")
        wrep = oTf[:, 0:384].rearrange("p (k a i) -> p k a i", k=TAPS, a=PH)
        dv = oTf[:, 384:768].rearrange("p (n l b) -> p n l b", n=3, l=NL)
        dd = oTf[:, 768:896].rearrange("p (l b) -> p l b", l=NL)
        sq = oTf[0:32, 896:1024].rearrange("p (l b) -> p l b", l=NL)
        mwT = kmf[0:STYLE, 0:512].rearrange("p (l a i) -> p l a i", l=NL, a=PH)
        w2sum = kmf[0:32, 512:1024].rearrange("p (l a i) -> p l a i", l=NL, a=PH)
        w2sq = kmf[0:32, 1024:1280].rearrange("p (n l i) -> p n l i", n=2, l=NL)
        d4diag = qT[0:32, :, :, :].rearrange("p a b c -> p (a b c)").rearrange("p (b o) -> p b o", b=B)
        kff = wqkvT[:, :, 0:L]
        yout = xs[:, :, :, :].rearrange("p n s m -> p n (s m)")

        acc_ready = sem("acc_ready")
        const_in, x_in = sem("const_in"), [sem(f"x_in{i}") for i in range(G)]
        chain_in = [sem(f"chain_in{i}") for i in range(2)]
        wide_in, wqkv_in, wo_in, kff_in, lora_in = (sem(n) for n in ("wide_in", "wqkv_in", "wo_in", "kff_in", "lora_in"))
        zeros = sem("zeros")
        xs_ready = sem("xs_ready")
        xp_in = [sem(f"xp_in{i}") for i in range(HG)]
        z1_ready, z2_ready, z3_ready = sem("z1_ready"), sem("z2_ready"), sem("z3_ready")
        z2_fixed, halo_ready = sem("z2_fixed"), sem("halo_ready")
        ct_ready, q_ready, k_ready, v_ready = (sem(n) for n in ("ct_ready", "q_ready", "k_ready", "v_ready"))
        scored, added, pv_half, cleared = sem("scored"), sem("added"), sem("pv_half"), sem("cleared")
        km_ready = sem("km_ready")
        shifted, exp_done, pblk_ready = sem("shifted"), sem("exp_done"), sem("pblk_ready")
        oT_ready, x1_ready, xf_ready = sem("oT_ready"), sem("x1_ready"), sem("xf_ready")
        ax_ready, bt_ready, y_ready = sem("ax_ready"), sem("bt_ready"), sem("y_ready")
        y_out = [sem(f"y_out{i}") for i in range(2)]
        dve_done, act_done, pool_done = sem("dve_done"), sem("act_done"), sem("pool_done")
        prep = sem("prep")
        sqrt_ready, var_ready = sem("sqrt_ready"), sem("var_ready")
        toep = [sem(f"toep{i}") for i in range(2)]
        wprep = sem("wprep")
        lprep = sem("lprep")

        def convs(c, h):
            a, b, cc, d = range(4 * h, 4 * h + 4)
            return ([("L1", c, g) for g in (a, b, cc, d)] + [("L2", c, a), ("L2", c, b), ("L3", c, a), ("L3", c, b),
                    ("L2", c, cc), ("L2", c, d), ("L4", c, a), ("L4", c, b), ("L3", c, cc), ("L3", c, d)],
                    [("L4", c, cc), ("L4", c, d)])

        def front(h):
            a, b, cc, d = range(4 * h, 4 * h + 4)
            return [("QKV", 0, a), ("QKV", 0, b), ("SC", 0, a), ("QKV", 0, cc), ("SC", 0, b), ("QKV", 0, d),
                    ("SC", 0, cc), ("SC", 0, d)]

        def back(h):
            return [(k, 0, g) for g in range(4 * h, 4 * h + 4) for k in ("PV", "OUT")]

        def ffn(h):
            return [("AX", 1, 4 * h)] + [s for g in range(4 * h, 4 * h + 4)
                                         for s in ([("AX", 1, g + 1)] if g % 4 < 3 else []) + [("Y", 1, g)]]

        order = [("PREP", 0, 0)]
        main, late = convs(0, 0)
        order += main + [("WT", 0, i) for i in range(NQKV + NT)] + late + [("LORA", 0, 0)] + [("PREP", 1, 0)] + front(0)
        main, late = convs(0, 1)
        order += main + back(0) + late + front(1)
        main, late = convs(1, 0)
        order += main + back(1) + late
        main, late = convs(1, 1)
        f0 = ffn(0)
        order += f0[:-3] + main + f0[-3:] + late + ffn(1)
        banks_of = {"PREP": 6, "L1": 1, "L2": 2, "L3": 2, "L4": 1, "WT": 1, "LORA": 10, "QKV": 3, "SC": 2, "PV": 1,
                    "OUT": 1, "AX": 1, "Y": 1}
        first_use, n = {}, 0
        for step in order:
            first_use[step] = n
            n += banks_of[step[0]]

        def bank(step, i=0):
            return acc[:, (first_use[step] + i) % BANKS, :]

        def take(pe, step, i=0):
            u = first_use[step] + i
            if u >= BANKS:
                reader, value = released[u - BANKS]
                pe.wait_ge(reader, value)
            return bank(step, i)

        def filled(eng, step, i=0):
            eng.wait_ge(acc_ready, first_use[step] + i + 1)
            return bank(step, i)

        def nth(c, g):
            return 8 * c + g + 1

        def readers(step):
            kind, c, g = step
            return {
                "PREP": lambda: [(prep, 4 * c + 2), (prep, 4 * c + 3), (prep, 4 * c + 3), (prep, 4 * c + 4),
                                 (toep[c], 1), (toep[c], 1)],
                "L1": lambda: [(z1_ready, nth(c, g))],
                "L2": lambda: [(z2_ready, 2 * nth(c, g) - 1), (z2_ready, 2 * nth(c, g))],
                "L3": lambda: [(z3_ready, 2 * nth(c, g) - 1), (z3_ready, 2 * nth(c, g))],
                "L4": lambda: [(ct_ready, nth(c, g))],
                "WT": lambda: [(wprep, g + 1)],
                "LORA": lambda: [(lprep, i + 2) for i in range(10)],
                "QKV": lambda: [(q_ready, g + 1), (k_ready, g + 1), (v_ready, g + 1)],
                "SC": lambda: [(scored, 2 * g + 1), (scored, 2 * g + 2)],
                "PV": lambda: [(oT_ready, g + 1)],
                "OUT": lambda: [(added, g + 1)],
                "AX": lambda: [(ax_ready, g + 1)],
                "Y": lambda: [(y_ready, g + 1)],
            }[kind]()

        released = [r for step in order for r in readers(step)]
        assert len(released) == n

        block = ctx.enter_context(nc.Block())

        @block.sync
        def _(sp):
            def load_chain(c):
                w, b, mw, mb = cw[c], cb[c], cmw[c], cmb[c]
                sp.dma_start(wnat[:, :], w.rearrange("l o i k -> (l o) (i k)")).then_inc(chain_in[c], 16)
                sp.dma_start(mwnat[:, :], mw.rearrange("l i s -> (l i) s")).then_inc(chain_in[c], 16)
                for p in range(PH):
                    sp.dma_start(w2rep[32 * p:32 * p + 32, :], w[1].rearrange("o i k -> o (i k)")).then_inc(chain_in[c], 16)
                    sp.dma_start(mbr[32 * p:32 * p + 32, c, :], mb.rearrange("l i -> i l"), allow_slow_non_contiguous=True).then_inc(chain_in[c], 16)
                    sp.dma_start(cbr[32 * p:32 * p + 32, c, :], b.rearrange("l i -> i l"), allow_slow_non_contiguous=True).then_inc(chain_in[c], 16)
                sp.dma_start(b4row[:, c, :], b[3].partition_broadcast(128)).then_inc(chain_in[c], 16)

            sp.dma_start(styn[:, :], style).then_inc(const_in, 16)
            sp.dma_start(const[:, :], consts).then_inc(const_in, 16)
            load_chain(0)
            for g in range(G):
                sp.dma_start(xres[:, g, :], x[GB * g:GB * g + GB].rearrange("b c l -> (b c) l")).then_inc(x_in[g], 16)

            def to_phases(c, g):
                sp.wait_ge(xs_ready, nth(c, g))
                if nth(c, g) > HG:
                    before = nth(c, g) - HG - 1
                    sp.wait_ge(acc_ready, first_use[("L2", before // G, before % G)] + 2)
                for p in range(PH):
                    for b in range(GB):
                        sp.dma_start(xp[32 * p:32 * p + 32, g % HG, b, 1:1 + M],
                                     xs[32 * b:32 * b + 32, g % 2, p, :]).then_inc(xp_in[g % HG], 16)

            for g in range(HG):
                to_phases(0, g)
            sp.dma_start(wq_nat, w_qkv[0:2 * L].rearrange("(t p) l -> p t l", p=128)).then_inc(wqkv_in, 16)
            sp.dma_start(wv_nat, w_qkv[2 * L:3 * L].rearrange("(t p) l -> p t l", p=128)).then_inc(wqkv_in, 16)
            sp.dma_start(wo_nat, w_out.rearrange("(t p) l -> p t l", p=128)).then_inc(wo_in, 16)
            sp.dma_start(la_nat, lora_a.rearrange("(t n) r l -> (n r) t l", n=4)).then_inc(lora_in, 16)
            for t in range(4):
                sp.dma_start(lb_nat[:, t], lora_b.rearrange("n (t p) r -> t p n r", p=128)[t]).then_inc(lora_in, 16)
            sp.dma_start(las_nat, lora_as).then_inc(lora_in, 16)
            sp.dma_start(lbs_nat, lora_bs.rearrange("(t p) r -> p t r", p=128)).then_inc(lora_in, 16)
            for t in range(NT):
                for j in range(4):
                    sp.dma_start(gsm[32 * j:32 * j + 32, t, :],
                                 gate[:, 4 * t + j].partition_broadcast(32), allow_slow_non_contiguous=True).then_inc(lora_in, 16)
            sp.dma_start(bqk[:, :], b_qkv[0:2 * L].rearrange("(t p) -> p t", p=128), allow_slow_non_contiguous=True).then_inc(wide_in, 16)
            sp.dma_start(bv_row, b_qkv[2 * L:3 * L].partition_broadcast(128)).then_inc(wide_in, 16)
            sp.dma_start(bo_row, b_out.partition_broadcast(128)).then_inc(wide_in, 16)
            sp.dma_start(bf_row, ffn_b.partition_broadcast(128)).then_inc(wide_in, 16)
            for g in range(HG, G):
                to_phases(0, g)
            sp.wait_ge(toep[0], 1)
            load_chain(1)
            for g in range(G):
                to_phases(1, g)
                if g == HG - 1:
                    sp.wait_ge(acc_ready, first_use[("QKV", 0, G - 1)] + 3)
                    sp.dma_start(kff, ffn_w.rearrange("(m s) o -> m s o", s=PH)).then_inc(kff_in, 16)
            for g in range(G):
                sp.wait_ge(y_ready, g + 1)
                sp.dma_start(out[GB * g:GB * g + GB].rearrange("b c l -> (b c) l"), yout[:, g % 2, :]).then_inc(y_out[g % 2], 16)
            for i in range(2):
                sp.wait_ge(y_out[i], 16 * (G // 2))

        @block.tensor
        def _(pe):
            mm, tr = nc.tensor.matmul, nc.tensor.transpose

            def prepare(step, c):
                pe.wait_ge(const_in, 32)
                pe.wait_ge(chain_in[c], 16 * 15)
                a = take(pe, step, 0)
                tr(a[0:STYLE, 0:32], styn[:, :], ident[0:32, 0:32])
                tr(a[0:STYLE, 32:160], mwnat[:, :], ident).then_inc(acc_ready, 1)
                a = take(pe, step, 1)
                pe.wait_ge(prep, 4 * c + 1)
                for k in range(TAPS):
                    kr = TAPS - 1 - k
                    last = tr(a[:, 128 * kr:128 * kr + 128], wrep[:, k].rearrange("p a b -> p (a b)"), ident)
                last.then_inc(acc_ready, 1)
                a = take(pe, step, 2)
                pe.wait_ge(prep, 4 * c + 2)
                for l in range(NL):
                    last = mm(a[:, 32 * l:32 * l + 32], mwT[:, l].rearrange("p a b -> p (a b)"), styT[:, :], start=True, stop=True)
                last.then_inc(acc_ready, 1)
                a = take(pe, step, 3)
                pe.wait_ge(prep, 4 * c + 3)
                for l in range(NL):
                    last = mm(a[:, 32 * l:32 * l + 32], w2sum[:, l].rearrange("p a b -> p (a b)"), sq[:, l, :],
                              start=True, stop=True)
                last.then_inc(acc_ready, 1)
                pe.wait_ge(prep, 4 * c + 4)
                for i in range(2):
                    a = take(pe, step, 4 + i)
                    mm(a, scale32[:, :], d4diag[:, 16 * i:16 * i + 16, :].rearrange("p a b -> p (a b)"),
                       start=True, stop=True).then_inc(acc_ready, 1)

            def layer1(step, c, g):
                a = take(pe, step)
                pe.wait_ge(xp_in[g % HG], 16 * 16 * (2 * c + g // HG + 1))
                src = xp[:, g % HG]
                mm(a, t1[:, c].rearrange("p a b -> p (a b)"), src[:, :, 1:1 + M], start=True, stop=False, skip_group_check=True)
                mm(a[0:32, :], wT[96:128, c, 2, 0, :], src[96:128, :, 0:M], start=False, stop=False,
                   tile_position=(96, 0), skip_group_check=True)
                mm(a[96:128, :], wT[0:32, c, 0, 0, :], src[0:32, :, 2:2 + M], start=False, stop=True,
                   tile_position=(0, 96), skip_group_check=True).then_inc(acc_ready, 1)

            def layer2(step, c, g):
                a, b = take(pe, step, 0), take(pe, step, 1)
                pe.wait_ge(z1_ready, nth(c, g))
                src = z1[:, g % HG]
                mm(a, t2[:, c, 0].rearrange("p a b -> p (a b)"), src[:, :, 1:1 + M], start=True, stop=False, skip_group_check=True)
                mm(b, t2[:, c, 1].rearrange("p a b -> p (a b)"), src[:, :, 1:1 + M], start=True, stop=False, skip_group_check=True)
                mm(a[0:64, :], taps2[96:128, c, 4:6, :].rearrange("p a b -> p (a b)"), src[96:128, :, 0:M], start=False, stop=True,
                   tile_position=(96, 0), skip_group_check=True).then_inc(acc_ready, 1)
                mm(b[64:128, :], taps2[0:32, c, 0:2, :].rearrange("p a b -> p (a b)"), src[0:32, :, 2:2 + M], start=False, stop=True,
                   tile_position=(0, 64), skip_group_check=True).then_inc(acc_ready, 1)

            def layer3(step, c, g):
                a, b = take(pe, step, 0), take(pe, step, 1)
                pe.wait_ge(z2_fixed, nth(c, g))
                sa, sb_ = z2[:, 0, g % 2], z2[:, 1, g % 2]
                w = t3[:, c].rearrange("p a b -> p (a b)")
                mm(a, w, sa[:, :, 1:1 + M], start=True, stop=False, skip_group_check=True)
                mm(b, w, sb_[:, :, 1:1 + M], start=True, stop=False, skip_group_check=True)
                before, after = wT[96:128, c, 2, 2, :], wT[0:32, c, 0, 2, :]
                mm(a[0:32, :], before, sb_[96:128, :, 0:M], start=False, stop=False, tile_position=(96, 0), skip_group_check=True)
                mm(b[96:128, :], after, sa[0:32, :, 2:2 + M], start=False, stop=False, tile_position=(0, 96), skip_group_check=True)
                mm(b[0:32, :], before, sa[96:128, :, 1:1 + M], start=False, stop=False, tile_position=(96, 0), skip_group_check=True)
                mm(a[96:128, :], after, sb_[0:32, :, 1:1 + M], start=False, stop=True, tile_position=(0, 96),
                   skip_group_check=True).then_inc(acc_ready, 2)

            def layer4(step, c, g):
                a = take(pe, step)
                pe.wait_ge(halo_ready, nth(c, g))
                for b in range(GB):
                    o = a[:, 128 * b:128 * b + 128]
                    for i, z in enumerate((z3[:, 0, g % 2, b, 1:1 + M], z3[:, 1, g % 2, b, 1:1 + M], halo[:, g % 2, b, :])):
                        last = mm(o, z, t4[:, c, i].rearrange("p a b -> p (a b)"), start=i == 0, stop=i == 2)
                last.then_inc(acc_ready, 1)

            def transpose_weight(step, i):
                a = take(pe, step)
                if i < NQKV:
                    pe.wait_ge(wqkv_in, 32)
                    nat = wq_nat[:, i, :] if i < 8 else wv_nat[:, i - 8, :]
                    nat = nat.rearrange("p (m s) -> p s m", s=PH)
                    for s in range(PH):
                        last = tr(a[:, 128 * s:128 * s + 128], nat[:, s, :], ident)
                else:
                    pe.wait_ge(wo_in, 16)
                    t = i - NQKV
                    for o in range(4):
                        last = tr(a[:, 128 * o:128 * o + 128], wo_nat[:, o, 128 * t:128 * t + 128], ident)
                last.then_inc(acc_ready, 1)

            def lora(step):
                pe.wait_ge(lora_in, 16 * (1 + 4 + 2 + 16))
                for t in range(4):
                    a = take(pe, step, t)
                    for o in range(4):
                        last = tr(a[:, 128 * o:128 * o + 128], lb_nat[:, o, 4 * t:4 * t + 4, :].rearrange("p n r -> p (n r)"), ident)
                    last.then_inc(acc_ready, 1)
                pe.wait_ge(lprep, 1)
                for i in range(2):
                    a = take(pe, step, 4 + i)
                    for half in range(2):
                        s = 2 * i + half
                        for t in range(4):
                            lhs = la_nat[:, t, :].rearrange("p (m s) -> p s m", s=PH)[:, s, :]
                            last = mm(a[:, 256 * half:256 * half + 256], lhs, gmat[:, t].rearrange("p g r -> p (g r)"),
                                      start=t == 0, stop=t == 3)
                    last.then_inc(acc_ready, 1)
                a = take(pe, step, 6)
                for s in range(PH):
                    last = tr(a[:, 32 * s:32 * s + 32], las_nat.rearrange("p (m s) -> p s m", s=PH)[:, s, :], ident[0:32, 0:32])
                last.then_inc(acc_ready, 1)
                a = take(pe, step, 7)
                for t in range(4):
                    last = tr(a[0:32, 128 * t:128 * t + 128], lbs_nat[:, t, :], ident)
                last.then_inc(acc_ready, 1)
                pe.wait_ge(lprep, 5)
                for h in range(2):
                    a = take(pe, step, 8 + h)
                    for t in range(4):
                        last = mm(a, gmat[:, t, 4 * h:4 * h + 4, :].rearrange("p g r -> p (g r)"), lbT[:, t, :], start=t == 0, stop=t == 3)
                    last.then_inc(acc_ready, 1)

            def qkv(step, g):
                if g == 0:
                    pe.wait_ge(wprep, NQKV)
                pe.wait_ge(ct_ready, nth(0, g))
                src = cT[:, g % HG]
                for i in range(2):
                    a = take(pe, step, i)
                    for t in range(NT):
                        for s in range(PH):
                            col = (NT * i + t) * 128
                            last = mm(a[:, 128 * t:128 * t + 128], wqkvT[:, s, col:col + 128], src[:, s, :], start=s == 0, stop=s == 3)
                    last.then_inc(acc_ready, 1)
                a = take(pe, step, 2)
                for s in range(PH):
                    last = mm(a, src[:, s, :], wqkvT[:, s, 2 * L:3 * L], start=s == 0, stop=s == 3)
                last.then_inc(acc_ready, 1)

            def scores(step, g):
                a = [take(pe, step, 0), take(pe, step, 1)]
                pe.wait_ge(q_ready, g + 1)
                for t in range(NT):
                    pe.wait_ge(km_ready, 2 * g + t // 2 + 1)
                    for r2 in range(2):
                        for b in range(GB):
                            last = mm(a[r2][32 * b:32 * b + 32, 128 * t:128 * t + 128],
                                      qT[64 * r2:64 * r2 + 64, g % 2, t, 32 * b:32 * b + 32],
                                      km[64 * r2:64 * r2 + 64, t // 2, t % 2, :, 32 * b:32 * b + 32],
                                      start=True, stop=True, tile_position=(64 * r2, 32 * b))
                last.then_inc(acc_ready, 2)

            def values(step, g):
                a = take(pe, step)
                for r2 in range(2):
                    pe.wait_ge(pblk_ready, 2 * g + r2 + 1)
                    for t in range(NT):
                        for e in range(2):
                            for j in (2 * r2, 2 * r2 + 1):
                                col = (8 * t + 2 * j) * HD
                                last = mm(a[32 * j:32 * j + 32, 128 * t:128 * t + 128], v2[:, g % HG, e, col:col + 32],
                                          pblk[:, r2, 4 * t + 2 * (j % 2) + e, :], start=e == 0, stop=e == 1,
                                          tile_position=(0, 32 * j))
                    if r2 == 0:
                        last.then_inc(pv_half, 1)
                last.then_inc(acc_ready, 1)

            def output(step, g):
                a = take(pe, step)
                if g == 0:
                    pe.wait_ge(wprep, NQKV + NT)
                pe.wait_ge(oT_ready, g + 1)
                for t in range(NT):
                    last = mm(a, oT[:, g % 2, 128 * t:128 * t + 128], woT[:, t, :], start=t == 0, stop=t == NT - 1)
                last.then_inc(acc_ready, 1)

            def low_rank(step, g):
                a = take(pe, step)
                if g == 0:
                    pe.wait_ge(lprep, 11)
                pe.wait_ge(ct_ready, nth(1, g))
                for s in range(PH):
                    for i, gi in enumerate((g, G)):
                        last = mm(a[32 * i:32 * i + 32, 0:128], aT[:, s, gi, :], cT[:, g % HG, s, :], start=s == 0, stop=s == 3,
                                  tile_position=(0, 32 * i))
                last.then_inc(acc_ready, 1)

            def feed_forward(step, g):
                a = take(pe, step)
                if g == 0:
                    pe.wait_ge(kff_in, 16)
                for s in range(PH):
                    mm(a, cT[:, g % HG, s, :], kff[:, s, :], start=s == 0, stop=False)
                pe.wait_ge(ax_ready, g + 1)
                pe.wait_ge(bt_ready, g + 1)
                mm(a, axT[:, g % 2, :], bT[:, g % 2, :], start=False, stop=True).then_inc(acc_ready, 1)

            for step in order:
                kind, c, g = step
                if kind == "PREP":
                    prepare(step, c)
                elif kind == "L1":
                    if g == 0:
                        pe.wait_ge(toep[c], 1)
                        pe.wait_ge(zeros, 1)
                    layer1(step, c, g)
                elif kind == "L2":
                    layer2(step, c, g)
                elif kind == "L3":
                    layer3(step, c, g)
                elif kind == "L4":
                    layer4(step, c, g)
                elif kind == "WT":
                    transpose_weight(step, g)
                elif kind == "LORA":
                    lora(step)
                elif kind == "QKV":
                    qkv(step, g)
                elif kind == "SC":
                    scores(step, g)
                elif kind == "PV":
                    values(step, g)
                elif kind == "OUT":
                    output(step, g)
                elif kind == "AX":
                    low_rank(step, g)
                else:
                    feed_forward(step, g)

        @block.scalar
        def _(act):
            def scaled(dst, step, i, c, g, layer, tile_rows=None):
                a = filled(act, step, i)
                for b in range(GB):
                    at = GB * g + b
                    last = nc.scalar.activation(dst[:, b, 1:1 + M], a[:, M * b:M * b + M], ACT.Identity,
                                                bias=tabB[:, c, layer, at:at + 1], scale=tabA[:, c, layer, at:at + 1])
                return last

            def exponentials(g):
                act.wait_ge(shifted, g + 1)
                nc.scalar.activation(S[:, g % HG, :], S[:, g % HG, :], ACT.Exp).then_inc(exp_done, 1)

            for n, step in enumerate(order):
                kind, c, g = step
                if kind == "PREP":
                    act.wait_ge(var_ready, c + 1)
                    nc.scalar.activation(dv[:, 1].rearrange("p a b -> p (a b)"), dv[:, 0].rearrange("p a b -> p (a b)"),
                                         ACT.Sqrt).then_inc(sqrt_ready, 1)
                elif kind == "L1":
                    if g == 0:
                        act.wait_ge(toep[c], 1)
                    scaled(z1[:, g % HG], step, 0, c, g, 0).then_inc(z1_ready, 1)
                    if order[n - 1][0] == "SC":
                        exponentials(order[n - 1][2])
                elif kind == "L2":
                    for i in range(2):
                        scaled(z2[:, i, g % 2], step, i, c, g, 1).then_inc(z2_ready, 1)
                elif kind == "L3":
                    for i in range(2):
                        scaled(z3[:, i, g % 2], step, i, c, g, 2).then_inc(z3_ready, 1)
                elif kind == "WT":
                    a = filled(act, step)
                    if g < NQKV:
                        dst = wqkvT[:, :, 128 * g:128 * g + 128]
                        src = a.rearrange("p (s o) -> p s o", s=PH)
                    else:
                        dst, src = woT[:, g - NQKV, :], a
                    nc.scalar.activation(dst, src, ACT.Copy).then_inc(wprep, 1)
                elif kind == "SC" and g % HG > 0:
                    exponentials(g - 1)
                elif kind == "PV":
                    a = filled(act, step)
                    nc.scalar.activation(oT[:, g % 2, :], a, ACT.Copy).then_inc(oT_ready, 1)
                elif kind == "AX":
                    a = filled(act, step)
                    nc.scalar.activation(axT[:, g % 2, :], a[0:64, 0:128], ACT.Copy).then_inc(ax_ready, 1)
                    if g >= 2:
                        act.wait_ge(acc_ready, first_use[("Y", 1, g - 2)] + 1)
                    if g == 0:
                        act.wait_ge(lprep, 11)
                    q = 32 * (g % 4)
                    nc.scalar.activation(bT[0:32, g % 2, :], bT4[q:q + 32, g // 4, :], ACT.Copy).then_inc(bt_ready, 1)

        @block.gpsimd
        def _(pool):
            tt = nc.gpsimd.tensor_tensor
            steps = [0]

            def after(ins):
                steps[0] += 1
                ins.then_inc(pool_done, 1)
                pool.wait_ge(pool_done, steps[0])

            for t in (t1, t2, t3, t4, taps2, taps4, xp, z2, z3):
                names = " ".join("abcd"[:len(t.shape) - 1])
                nc.gpsimd.memset(t[:].rearrange(f"p {names} -> p ({names})"), 0.0)
            nc.gpsimd.memset(scale32[:, :], SCALE).then_inc(zeros, 1)
            pool.wait_ge(zeros, 1)
            for step in order:
                kind, c, g = step
                if kind == "LORA":
                    pool.wait_ge(acc_ready, first_use[step] + 10)
                    nc.gpsimd.memset(pblk[:, :, :, :].rearrange("p a b c -> p (a b c)"), 0.0)
                    nc.gpsimd.memset(v2f, 0.0).then_inc(cleared, 1)
                    pool.wait_ge(cleared, 1)
                elif kind == "L2":
                    pool.wait_ge(z2_ready, 2 * nth(c, g))
                    if g == 0:
                        pool.wait_ge(toep[c], 1)
                    at = slice(GB * g, GB * g + GB)
                    first, last = z2[0:32, 0, g % 2, :, 1], z2[96:128, 1, g % 2, :, M]
                    after(tt(first, first, edge[0:32, c, at], ALU.subtract))
                    tt(last, last, edge[96:128, c, at], ALU.subtract).then_inc(z2_fixed, 1)
                    pool.wait_ge(z2_fixed, nth(c, g))
                elif kind == "L3":
                    if nth(c, g) > 2:
                        before = nth(c, g) - 3
                        pool.wait_ge(acc_ready, first_use[("L4", before // G, before % G)] + 1)
                    pool.wait_ge(z3_ready, 2 * nth(c, g))
                    after(nc.gpsimd.tensor_copy(halo[0:64, g % 2], z3[0:64, 0, g % 2, :, 2:2 + M]))
                    nc.gpsimd.tensor_copy(halo[64:128, g % 2], z3[64:128, 1, g % 2, :, 0:M]).then_inc(halo_ready, 1)
                    pool.wait_ge(halo_ready, nth(c, g))
                elif kind == "QKV":
                    pool.wait_ge(k_ready, g + 1)
                    if g >= 1:
                        pool.wait_ge(acc_ready, first_use[("SC", 0, g - 1)] + 2)
                    mask = const[:, C_MASK:C_MASK + 4].unsqueeze(2).broadcast_to((128, 4, 128))
                    for t in range(NT):
                        masked = tt(km[:, t // 2, t % 2], kT[:, g % 2, t, :].unsqueeze(1).broadcast_to((128, 4, 128)), mask, ALU.mult)
                        if t % 2:
                            masked.then_inc(km_ready, 1)
                            pool.wait_ge(km_ready, 2 * g + t // 2 + 1)
                        else:
                            after(masked)
                elif kind == "OUT":
                    pool.wait_ge(xs_ready, nth(1, g))
                    tt(xres[:, g, :], xres[:, g, :], bf_row, ALU.add).then_inc(xf_ready, 1)
                    pool.wait_ge(xf_ready, g + 1)

        @block.vector
        def _(dve):
            v = nc.vector
            tt, stt, ts, copy = v.tensor_tensor, v.scalar_tensor_tensor, v.tensor_scalar, v.tensor_copy
            links = [0]

            def link(ins):
                links[0] += 1
                ins.then_inc(dve_done, 1)
                dve.wait_ge(dve_done, links[0])

            def scale_input(c, g):
                if nth(c, g) > 2:
                    before = nth(c, g) - 3
                    dve.wait_ge(xp_in[before % HG], 16 * 16 * (before // HG + 1))
                ts(xs[:, g % 2], xres[:, g, :].rearrange("p (m s) -> p s m", s=PH), sin[:, c, g:g + 1], None,
                   ALU.mult).then_inc(xs_ready, 1)

            def prepare(step, c):
                dve.wait_ge(chain_in[c], 16 * 15)
                if c == 0:
                    dve.wait_ge(const_in, 32)
                    dve.wait_ge(zeros, 1)
                src = wnat[:, :].rearrange("p (i k) -> p k i", k=TAPS)
                for k in range(TAPS):
                    last = copy(wrep[:, k], src[:, k, :].unsqueeze(1).broadcast_to((128, PH, C)))
                last.then_inc(prep, 1)
                a = filled(dve, step, 0)
                copy(styT[:, :], a[0:STYLE, 0:32])
                copy(mwT[:, :, :, :], a[0:STYLE, 32:160].rearrange("p (l i) -> p l i", l=NL).unsqueeze(2)
                     .broadcast_to((STYLE, NL, PH, C))).then_inc(prep, 1)
                w2k = w2rep[:, :].rearrange("p (i k) -> p k i", k=TAPS)
                for j in range(4):
                    dst = taps2[:, c, 3 - j:6 - j, :]
                    link(stt(dst, w2k, 2.0 * BLUR[j], dst, ALU.mult, ALU.add))
                a = filled(dve, step, 1)
                link(copy(wT[:, c].rearrange("p k l o -> p (k l o)"), a[:, 0:TAPS * 128]))
                wt = [wT[0:32, c, k] for k in range(TAPS)]
                link(tt(w2sq[:, 0], wt[0], wt[0], ALU.mult))
                link(tt(w2sq[:, 1], wt[1], wt[1], ALU.mult))
                link(tt(w2sq[:, 0], w2sq[:, 0], w2sq[:, 1], ALU.add))
                link(tt(w2sq[:, 1], wt[2], wt[2], ALU.mult))
                link(tt(w2sq[:, 0], w2sq[:, 0], w2sq[:, 1], ALU.add))
                copy(w2sum[:, :, :, :], w2sq[:, 0].unsqueeze(2).broadcast_to((32, NL, PH, C)))
                a = filled(dve, step, 2)
                link(tt(stab[:, :, :], a[:, 0:NL * B].rearrange("p (l b) -> p l b", l=NL),
                        mbr[:, c, :].unsqueeze(2).broadcast_to((128, NL, B)), ALU.add))
                tt(sq[:, :, :], stab[0:32], stab[0:32], ALU.mult).then_inc(prep, 1)
                for j in range(GB):
                    last = copy(sin[32 * j:32 * j + 32, c, :], stab[32 * j:32 * j + 32, 0, :].rearrange("p (g j) -> p j g", j=GB)[:, j, :])
                link(last)
                if c == 0:
                    for g in range(HG):
                        if g < 2:
                            dve.wait_ge(x_in[g], 16)
                            scale_input(0, g)
                a = filled(dve, step, 3)
                flat = [dv[:, i].rearrange("p a b -> p (a b)") for i in range(3)]
                ts(flat[0], a[:, 0:NL * B], SCALE * SCALE, EPS, ALU.mult, ALU.add).then_inc(var_ready, 1)
                dve.wait_ge(sqrt_ready, c + 1)
                d = dd[:, :, :].rearrange("p a b -> p (a b)")
                link(v.reciprocal(flat[1], flat[1]))
                link(tt(flat[2], flat[1], flat[1], ALU.mult))
                link(tt(flat[2], flat[2], flat[0], ALU.mult))
                link(ts(flat[2], flat[2], -0.5, 1.5, ALU.mult, ALU.add))
                link(tt(d, flat[1], flat[2], ALU.mult))
                tt(d4diag[:, :, :], dd[0:32, 3, :].unsqueeze(2).broadcast_to((32, B, C)),
                   const[0:32, C_SEL:C_SEL + C].unsqueeze(1).broadcast_to((32, B, C)), ALU.mult).then_inc(prep, 1)
                b = [cbr[:, c, l:l + 1] for l in range(NL)]
                stt(tabA[:, c, 0, :], dd[:, 0, :], SCALE, dd[:, 1, :], ALU.mult, ALU.mult)
                ts(tabB[:, c, 0, :], dd[:, 1, :], b[0], None, ALU.mult)
                stt(tabA[:, c, 1, :], stab[:, 1, :], SCALE, stab[:, 2, :], ALU.mult, ALU.mult)
                ts(tabB[:, c, 1, :], stab[:, 2, :], b[1], 2.0, ALU.mult, ALU.mult)
                ts(edge[:, c, :], stab[:, 2, :], b[1], 2.0 * BLUR_EDGE, ALU.mult, ALU.mult)
                stt(tabA[:, c, 2, :], dd[:, 2, :], SCALE, stab[:, 3, :], ALU.mult, ALU.mult)
                ts(tabB[:, c, 2, :], stab[:, 3, :], b[2], None, ALU.mult)
                for j in range(4):
                    dst = taps4[:, c, 3 - j:6 - j, :]
                    link(stt(dst, wT[:, c, :, 3, :], BLUR[j], dst, ALU.mult, ALU.add))
                for p in range(PH):
                    q = slice(32 * p, 32 * p + 32)
                    lo, hi = max(0, p - 1), min(PH, p + 2)
                    copy(t1[q, c, lo:hi, :], wT[q, c, lo - p + 1:hi - p + 1, 0, :])
                    copy(t3[q, c, lo:hi, :], wT[q, c, lo - p + 1:hi - p + 1, 2, :])
                    lo, hi = max(0, 2 * p - 2), min(8, 2 * p + 4)
                    copy(t2[q, c].rearrange("p t n i -> p (t n) i")[:, lo:hi, :], taps2[q, c, lo - 2 * p + 2:hi - 2 * p + 2, :])
                    for i, n in enumerate((p, p + 4, p + 8 if p < 2 else p - 4)):
                        ss = [s for s in range(PH) if 0 <= 3 - n + 2 * s <= 5]
                        r0 = 3 - n + 2 * ss[0]
                        copy(t4[q, c, i, ss[0]:ss[-1] + 1, :], taps4[q, c, r0:r0 + 2 * len(ss) - 1:2, :])
                for i in range(2):
                    a = filled(dve, step, 4 + i)
                    last = copy(d4row[:, c, 16 * i:16 * i + 16, :].rearrange("p b o -> p (b o)"), a)
                last.then_inc(toep[c], 1)

            def lora(step):
                dve.wait_ge(lora_in, 16 * (1 + 4 + 2 + 16))
                sel = const[:, C_SEL:C_SEL + C].unsqueeze(1).broadcast_to((128, G, RANK))
                for t in range(4):
                    last = tt(gmat[:, t], gsm[:, t, :].unsqueeze(2).broadcast_to((128, G, RANK)), sel, ALU.mult)
                last.then_inc(lprep, 1)
                for t in range(4):
                    a = filled(dve, step, t)
                    copy(lbT[:, t, :], a).then_inc(lprep, 1)
                for i in range(2):
                    a = filled(dve, step, 4 + i)
                    copy(aT[:, 2 * i:2 * i + 2, 0:G, :], a.rearrange("p (s g r) -> p s g r", s=2, g=G)).then_inc(lprep, 1)
                a = filled(dve, step, 6)
                copy(aT[:, :, G, :], a[:, 0:PH * RANK].rearrange("p (s r) -> p s r", s=PH)).then_inc(lprep, 1)
                a = filled(dve, step, 7)
                copy(bT[32:64, 0, :], a[0:32, :])
                copy(bT[32:64, 1, :], a[0:32, :]).then_inc(lprep, 1)
                for h in range(2):
                    a = filled(dve, step, 8 + h)
                    copy(bT4[:, h, :], a).then_inc(lprep, 1)

            def down_out(step, c, g):
                a = filled(dve, step)
                view = cT[:, g % HG].rearrange("p s (b o) -> p b s o", b=GB)
                for b in range(GB):
                    last = tt(view[:, b], a[:, 128 * b:128 * b + 128].rearrange("p (s o) -> p s o", s=PH),
                              d4row[:, c, GB * g + b, :].unsqueeze(1).broadcast_to((128, PH, C)), ALU.mult)
                link(last)
                flat = cT[:, g % HG].rearrange("p s (b o) -> p (s b) o", b=GB)
                tt(flat, flat, b4row[:, c, :].unsqueeze(1).broadcast_to((128, PH * GB, C)), ALU.add).then_inc(ct_ready, 1)

            def qkv(step, g):
                if g == 0:
                    dve.wait_ge(wide_in, 64)
                    dve.wait_ge(cleared, 1)
                for i, (dst, ready) in enumerate(((qT, q_ready), (kT, k_ready))):
                    a = filled(dve, step, i)
                    tt(dst[:, g % 2], a.rearrange("p (t n) -> p t n", t=NT),
                       bqk[:, NT * i:NT * i + NT].unsqueeze(2).broadcast_to((128, NT, 128)), ALU.add).then_inc(ready, 1)
                a = filled(dve, step, 2)
                for e in range(2):
                    pick = lambda ap: ap.rearrange("p (n e d) -> p e n d", e=2, d=HD)[:, e]
                    last = tt(pick(v2[:, g % HG, e, :]), pick(a), pick(bv_row), ALU.add)
                last.then_inc(v_ready, 1)

            def scores(step, g):
                for i in range(2):
                    a = filled(dve, step, i)
                    half = slice(512 * i, 512 * i + 512)
                    stt(S[:, g % HG, half], a, QK_SCALE, const[:, C_ALIBI + 512 * i:C_ALIBI + 512 * i + 512], ALU.mult,
                        ALU.add).then_inc(scored, 1)
                dve.wait_ge(scored, 2 * g + 2)
                rows_ = S[:, g % HG, :].rearrange("p (h k) -> p h k", k=C)
                link(v.tensor_reduce(stat[:, 0, g % HG, :], rows_, AX_X, ALU.max))
                tt(rows_, rows_, stat[:, 0, g % HG, :].unsqueeze(2).broadcast_to((128, HEADS, C)), ALU.subtract).then_inc(shifted, 1)

            def normalise(g):
                dve.wait_ge(exp_done, g + 1)
                rows_ = S[:, g % HG, :].rearrange("p (h k) -> p h k", k=C)
                link(v.tensor_reduce(stat[:, 1, g % HG, :], rows_, AX_X, ALU.add))
                link(v.reciprocal(stat[:, 1, g % HG, :], stat[:, 1, g % HG, :]))
                link(tt(rows_, rows_, stat[:, 1, g % HG, :].unsqueeze(2).broadcast_to((128, HEADS, C)), ALU.mult))

            def turn(g):
                for r2 in range(2):
                    if g >= 1:
                        if r2 == 0:
                            dve.wait_ge(pv_half, g)
                        else:
                            dve.wait_ge(acc_ready, first_use[("PV", 0, g - 1)] + 1)
                    for b in range(GB):
                        q = slice(32 * b, 32 * b + 32)
                        last = v.transpose(pblk[q, r2, :, 32 * b:32 * b + 32],
                                           S[q, g % HG, 512 * r2:512 * r2 + 512].rearrange("p (h k) -> p h k", k=C))
                    last.then_inc(pblk_ready, 1)

            def residual(step, g):
                a = filled(dve, step)
                tt(xres[:, g, :], xres[:, g, :], a, ALU.add).then_inc(added, 1)
                dve.wait_ge(added, g + 1)
                link(tt(xres[:, g, :], xres[:, g, :], bo_row, ALU.add))
                scale_input(1, g)

            def last_sum(step, g):
                a = filled(dve, step)
                dve.wait_ge(xf_ready, g + 1)
                if g >= 2:
                    dve.wait_ge(y_out[g % 2], 16 * (g // 2))
                else:
                    dve.wait_ge(xp_in[2 + g], 16 * 16 * 4)
                tt(yout[:, g % 2, :], a, xres[:, g, :], ALU.add).then_inc(y_ready, 1)

            for step in order:
                kind, c, g = step
                if kind == "PREP":
                    prepare(step, c)
                    if c == 0:
                        for g2 in (2, 3):
                            dve.wait_ge(x_in[g2], 16)
                            scale_input(0, g2)
                elif kind == "L2" and (c, g) == (0, 2):
                    dve.wait_ge(x_in[4], 16)
                    scale_input(0, 4)
                elif kind == "L2" and (c, g) == (0, 3):
                    dve.wait_ge(x_in[5], 16)
                    scale_input(0, 5)
                elif kind == "WT" and g in (0, 1):
                    dve.wait_ge(x_in[6 + g], 16)
                    scale_input(0, 6 + g)
                elif kind == "LORA":
                    lora(step)
                elif kind == "L4":
                    down_out(step, c, g)
                elif kind == "QKV":
                    qkv(step, g)
                elif kind == "SC":
                    scores(step, g)
                    if g % HG > 1:
                        normalise(g - 2)
                    if g % HG == 3:
                        normalise(g - 1)
                        normalise(g)
                        turn(g - 3)
                elif kind == "OUT":
                    residual(step, g)
                elif kind == "PV" and g % HG < 3:
                    turn(g + 1)
                elif kind == "Y":
                    last_sum(step, g)


_INS = ["x", "cond_512"] + [f"L0_{c}_{n}" for c in ("cond", "cond2") for n in ("weights", "biases", "mod_w", "mod_b")] + [
    "L0_attn_w_qkv", "L0_attn_b_qkv", "L0_attn_w_out", "L0_attn_b_out", "L0_ffn_gate", "L0_ffn_kernel", "L0_ffn_bias",
    "L0_ffn_lora_A", "L0_ffn_lora_B", "L0_ffn_lora_A_shared", "L0_ffn_lora_B_shared"]


def kernel(**inputs):
    import concourse.bacc as bacc
    from concourse.bass_utils import run_bass_kernel_spmd

    nc = bacc.Bacc("TRN2", target_bir_lowering=False, num_devices=1)
    arrays = {f"in_{n}": np.ascontiguousarray(inputs[n]) for n in _INS}
    arrays["in_consts"] = shape_constants()
    d = {n: nc.dram_tensor(n, a.shape, mybir.dt.from_np(a.dtype), kind="ExternalInput").ap() for n, a in arrays.items()}
    out = nc.dram_tensor("out", (B, C, L), F32, kind="ExternalOutput").ap()
    chain = [[d[f"in_L0_{c}_{n}"] for c in ("cond", "cond2")] for n in ("weights", "biases", "mod_w", "mod_b")]
    build(nc, d["in_x"], d["in_cond_512"], *chain, *[d[f"in_{n}"] for n in _INS[10:]], d["in_consts"], out)
    r = run_bass_kernel_spmd(nc, [arrays], core_ids=[0])
    return r.results[0]["out"]
```

```python
from contextlib import ExitStack

import numpy as np

import concourse.bass as bass
from concourse import mybir

F32 = mybir.dt.float32
ALU = mybir.AluOpType
ACT = mybir.ActivationFunctionType
AX_X = mybir.AxisListType.X

B, C, L = 32, 32, 512
STYLE = 64
TAPS, PH = 3, 4
M = L // PH
MP = M + 2
G, GB = 8, 4
HG = G // 2
NL = 4
HEADS, HD = 32, 16
NT = L // 128
NQKV = 3 * NT
LORAS, RANK = 16, 32
BANKS = 8
SCALE = 1.0 / float(np.sqrt(C * TAPS ** 2))
EPS = 1e-8
BLUR = [0.125, 0.375, 0.375, 0.125]
BLUR_EDGE = 0.125
QK_SCALE = 1.0 / float(np.sqrt(HD))

C_ALIBI, C_MASK = 0, HEADS * C
C_SEL = C_MASK + 8
N_CONST = C_SEL + C
W_T, W_UP, W_T1, W_T3 = 0, TAPS * NL * C, TAPS * NL * C + TAPS * C, TAPS * NL * C + TAPS * C + PH * C
W_CB = W_T3 + PH * C
W_B4, N_W = W_CB + NL, W_CB + NL + C
S_T, S_MB, N_S = NL * PH * C, NL * PH * C + B, NL * PH * C + B + NL


def shape_constants():
    out = np.zeros((128, N_CONST), np.float32)
    slopes = (1.0 / 2.0 ** (np.arange(1, HEADS + 1, dtype=np.float32) * np.float32(8.0 / HEADS))).astype(np.float32)
    k, q = np.arange(C), np.arange(128) % C
    for h in range(HEADS):
        bias = slopes[h] * (k - (C - 1)).astype(np.float32)
        out[:, C_ALIBI + C * h:C_ALIBI + C * h + C] = np.where(q[:, None] >= k[None, :], bias[None, :], np.float32(-1e9))
    for c in range(8):
        out[:, C_MASK + c] = np.arange(128) // HD == c
    out[:, C_SEL:C_SEL + C] = np.tile(np.eye(C), (4, 1))
    return out


def pack_chain(w, b, mw, mb, style):
    out = np.zeros((128, N_W), np.float32)
    proj = np.zeros((128, N_S), np.float32)
    wt = w.transpose(2, 3, 0, 1)[:, ::-1]
    out[:, W_T:W_T + TAPS * NL * C] = np.tile(wt.reshape(C, -1), (PH, 1))
    out[:, W_UP:W_UP + TAPS * C] = np.tile(w[1].transpose(0, 2, 1).reshape(C, -1), (PH, 1))
    for at, l in ((W_T1, 0), (W_T3, 2)):
        for p in range(PH):
            for s in range(max(0, p - 1), min(PH, p + 2)):
                out[C * p:C * p + C, at + C * s:at + C * s + C] = w[l, :, :, p - s + 1].T
    out[:, W_CB:W_CB + NL] = np.tile(b.T, (PH, 1))
    out[:, W_B4:W_B4 + C] = b[3][None, :]
    proj[:STYLE, :S_T] = np.tile(mw.transpose(2, 0, 1)[:, :, None, :], (1, 1, PH, 1)).reshape(STYLE, -1)
    proj[:STYLE, S_T:S_MB] = style.T
    proj[:, S_MB:] = np.tile(mb.T, (PH, 1))
    return out, proj


def build(nc, x, xph, chain_w, chain_s, w_qkvT, bqk_d, b_qkv, w_outT, b_out, gates, ffn_w, ffn_b,
          lora_a, lora_bT, lora_asT, lora_bsT, consts, out):
    ctx = ExitStack()
    with ctx:
        def sb(name, shape):
            return ctx.enter_context(nc.sbuf_tensor(name, shape, F32))

        def sem(name):
            return ctx.enter_context(nc.semaphore(name))

        acc = ctx.enter_context(nc.psum_tensor("acc", [128, BANKS, 512], F32))
        const = sb("const", [128, N_CONST])
        xres = sb("xres", [128, G, L])
        xs = sb("xs", [128, 2, PH, M])
        xp = sb("xp", [128, HG, GB, MP])
        z1 = xp
        z2 = sb("z2", [128, 2, 2, GB, MP])
        z3 = sb("z3", [128, 2, 2, GB, MP])
        halo = sb("halo", [128, 2, GB, M])
        cT = sb("cT", [128, HG, PH, 128])
        qT = sb("qT", [128, 2, NT, 128])
        kT = sb("kT", [128, 2, NT, 128])
        km = sb("km", [128, NT, 8, 128])
        v2 = sb("v2", [128, HG, 2, L])
        S = sb("S", [128, HG, HEADS * C])
        pblk = sb("pblk", [128, 2, 16, 128])
        stat = sb("stat", [128, 2, HG, HEADS])
        oT = sb("oT", [128, 2, NT * 128])
        wqkvT = sb("wqkvT", [128, PH, NQKV * 128])
        woT = sb("woT", [128, NT, L])
        bqk = sb("bqk", [128, 2 * NT])
        rows = sb("rows", [128, 3, L])
        bv_row, bo_row, bf_row = rows[:, 0, :], rows[:, 1, :], rows[:, 2, :]
        aT = sb("aT", [128, PH, G + 1, RANK])
        bT4 = sb("bT4", [128, 2, L])
        bT = sb("bT", [64, 2, L])
        axT = sb("axT", [64, 2, 128])

        chw = sb("chw", [128, N_W])
        chs = sb("chs", [128, N_S])
        wT = chw[:, W_T:W_UP].rearrange("p (k l o) -> p k l o", k=TAPS, l=NL)
        w_up = chw[:, W_UP:W_T1].rearrange("p (k i) -> p k i", k=TAPS)
        t1, t3 = chw[:, W_T1:W_T3], chw[:, W_T3:W_CB]
        cbr, b4row = chw[:, W_CB:W_B4], chw[:, W_B4:N_W]
        mwT = chs[0:STYLE, 0:S_T].rearrange("p (l n) -> p l n", l=NL)
        styT, mbr = chs[0:STYLE, S_T:S_MB], chs[:, S_MB:N_S]
        stab2 = sb("stab", [128, 2, NL, B])
        taps2 = sb("taps2", [128, 6, C])
        taps4 = sb("taps4", [128, 6, C])
        t2 = sb("t2", [128, 2, PH, C])
        t4 = sb("t4", [128, 3, PH, C])
        sin = sb("sin", [128, G])
        tabA = sb("tabA", [128, 3, B])
        tabB = sb("tabB", [128, 3, B])
        edge = sb("edge", [128, B])
        scale32 = sb("scale32", [32, 128])
        d4row = sb("d4row", [128, B, C])
        gsm = sb("gsm", [128, NT, G])

        v2f = v2[:, :, :, :].rearrange("p a b c -> p (a b c)")
        la_nat = v2f[:, 0:2048].rearrange("p (t l) -> p t l", t=4)
        kmf = km[:, :, :, :].rearrange("p a b c -> p (a b c)")
        lbT = kmf[:, 0:2048].rearrange("p (t l) -> p t l", t=4)
        gmat = qT[:, :, :, :].rearrange("p a b c -> p (a b c)").rearrange("p (t g r) -> p t g r", t=4, g=G)

        oTf = oT[:, :, :].rearrange("p a b -> p (a b)")
        dv = oTf[:, 384:768].rearrange("p (n l b) -> p n l b", n=3, l=NL)
        dd = oTf[:, 768:896].rearrange("p (l b) -> p l b", l=NL)
        sq = oTf[0:32, 896:1024].rearrange("p (l b) -> p l b", l=NL)
        w2sum = S[0:32, HG - 1, 0:512].rearrange("p (l a i) -> p l a i", l=NL, a=PH)
        w2sq = S[0:32, HG - 1, 512:768].rearrange("p (n l i) -> p n l i", n=2, l=NL)
        d4diag = xs[0:32, :, :, :].rearrange("p a b c -> p (a b c)").rearrange("p (b o) -> p b o", b=B)
        kff = wqkvT[:, :, 0:L]
        yout = xs[:, :, :, :].rearrange("p n s m -> p n (s m)")

        scratch = nc.dram_tensor("scratch", (G, 128, PH, M), F32, kind="Internal").ap()

        acc_ready = sem("acc_ready")
        const_in, x_in = sem("const_in"), [sem(f"x_in{i}") for i in range(G)]
        chs_in, chw_in = [sem(f"chs_in{i}") for i in range(2)], [sem(f"chw_in{i}") for i in range(2)]
        wide_in, wqkv_in, wo_in, kff_in, lora_in, gate_in = (
            sem(n) for n in ("wide_in", "wqkv_in", "wo_in", "kff_in", "lora_in", "gate_in"))
        zeros = sem("zeros")
        xs_ready = sem("xs_ready")
        xs_out = [sem(f"xs_out{i}") for i in range(2)]
        xp_in = [sem(f"xp_in{i}") for i in range(HG)]
        x_scaled = sem("x_scaled")
        z1_ready, z2_ready, z3_ready = sem("z1_ready"), sem("z2_ready"), sem("z3_ready")
        z2_fixed, halo_ready = sem("z2_fixed"), sem("halo_ready")
        ct_ready, q_ready, k_ready, v_ready = (sem(n) for n in ("ct_ready", "q_ready", "k_ready", "v_ready"))
        scored, added, pv_half, cleared = sem("scored"), sem("added"), sem("pv_half"), sem("cleared")
        km_ready = [sem(f"km_ready{t}") for t in range(NT)]
        shifted, exp_done, pblk_ready = sem("shifted"), sem("exp_done"), sem("pblk_ready")
        oT_ready, x1_ready, xf_ready = sem("oT_ready"), sem("x1_ready"), sem("xf_ready")
        ax_ready, bt_ready, y_ready = sem("ax_ready"), sem("bt_ready"), sem("y_ready")
        y_out = [sem(f"y_out{i}") for i in range(2)]
        dve_done, act_done, pool_done = sem("dve_done"), sem("act_done"), sem("pool_done")
        style_ready, sq_ready, var_read, diag_ready = (sem(n) for n in ("style_ready", "sq_ready", "var_read", "diag_ready"))
        sqrt_ready = sem("sqrt_ready")
        tab_ready, taps_ready, t2_ready, t4_ready, d4_ready = (
            sem(n) for n in ("tab_ready", "taps_ready", "t2_ready", "t4_ready", "d4_ready"))
        lprep = sem("lprep")

        def convs(c, h):
            a, b, cc, d = range(4 * h, 4 * h + 4)
            return ([("L1", c, a), ("L1", c, cc), ("L2", c, a), ("L2", c, b), ("L3", c, a), ("L3", c, b),
                    ("L2", c, cc), ("L2", c, d), ("L4", c, a), ("L4", c, b), ("L3", c, cc), ("L3", c, d)],
                    [("L4", c, cc), ("L4", c, d)])

        def front(h):
            a, b, cc, d = range(4 * h, 4 * h + 4)
            return [("QKV", 0, a), ("QKV", 0, b), ("SC", 0, a), ("QKV", 0, cc), ("SC", 0, b), ("QKV", 0, d),
                    ("SC", 0, cc)], [("SC", 0, d)]

        def back(h):
            return [(k, 0, g) for g in range(4 * h, 4 * h + 4) for k in ("PV", "OUT")]

        def ffn(h):
            return [("AX", 1, 4 * h)] + [s for g in range(4 * h, 4 * h + 4)
                                         for s in ([("AX", 1, g + 1)] if g % 4 < 3 else []) + [("Y", 1, g)]]

        main, late = convs(0, 0)
        order = [("PA", 0, 0), ("PB", 0, 0)] + main[:2] + [("PC", 0, 0)] + main[2:]
        order += [("LORA", 0, 0), ("PA", 1, 0)] + late
        fronts, last_scores = front(0)
        main, late = convs(0, 1)
        order += fronts + main[:3] + last_scores + main[3:] + back(0) + late
        fronts, last_scores = front(1)
        main, late = convs(1, 0)
        order += fronts[:2] + [("PB", 1, 0)] + fronts[2:4] + [("PC", 1, 0)] + fronts[4:]
        order += main[:3] + last_scores + main[3:] + back(1) + late
        main, late = convs(1, 1)
        f0 = ffn(0)
        order += f0[:-3] + main + f0[-3:] + late + ffn(1)
        banks_of = {"PA": 1, "PB": 1, "PC": 2, "L1": 2, "L2": 2, "L3": 2, "L4": 1, "LORA": 4, "QKV": 3, "SC": 2, "PV": 1,
                    "OUT": 1, "AX": 1, "Y": 1}
        first_use, n = {}, 0
        for step in order:
            first_use[step] = n
            n += banks_of[step[0]]

        exp_after, norm_after = {}, {}
        for at, (kind, _, g) in enumerate(order):
            if kind == "SC":
                exp_after.setdefault(at + (1 if g % HG < 3 else 2), []).append(g)
                norm_after.setdefault(at + (3 if g % HG < 3 else 4), []).append(g)

        def bank(step, i=0):
            return acc[:, (first_use[step] + i) % BANKS, :]

        def take(pe, step, i=0):
            u = first_use[step] + i
            if u >= BANKS:
                reader, value = released[u - BANKS]
                pe.wait_ge(reader, value)
            return bank(step, i)

        def filled(eng, step, i=0):
            eng.wait_ge(acc_ready, first_use[step] + i + 1)
            return bank(step, i)

        def nth(c, g):
            return 8 * c + g + 1

        def readers(step):
            kind, c, g = step
            return {
                "PA": lambda: [(style_ready, c + 1)],
                "PB": lambda: [(var_read, c + 1)],
                "PC": lambda: [(d4_ready, c + 1), (d4_ready, c + 1)],
                "L1": lambda: [(z1_ready, nth(c, g)), (z1_ready, nth(c, g + 1))],
                "L2": lambda: [(z2_ready, 2 * nth(c, g) - 1), (z2_ready, 2 * nth(c, g))],
                "L3": lambda: [(z3_ready, 2 * nth(c, g) - 1), (z3_ready, 2 * nth(c, g))],
                "L4": lambda: [(ct_ready, nth(c, g))],
                "LORA": lambda: [(lprep, i + 2) for i in range(4)],
                "QKV": lambda: [(q_ready, g + 1), (k_ready, g + 1), (v_ready, g + 1)],
                "SC": lambda: [(scored, 2 * g + 1), (scored, 2 * g + 2)],
                "PV": lambda: [(oT_ready, g + 1)],
                "OUT": lambda: [(added, g + 1)],
                "AX": lambda: [(ax_ready, g + 1)],
                "Y": lambda: [(y_ready, g + 1)],
            }[kind]()

        released = [r for step in order for r in readers(step)]
        assert len(released) == n

        block = ctx.enter_context(nc.Block())

        @block.sync
        def _(sp):
            def first_input(g):
                sp.dma_start(xp[:, g % HG, :, 1:1 + M], xph[g]).then_inc(xp_in[g % HG], 16)

            sp.dma_start(chs[:, :], chain_s[0]).then_inc(chs_in[0], 16)
            sp.dma_start(chw[:, :], chain_w[0]).then_inc(chw_in[0], 16)
            for g in range(HG):
                first_input(g)
            sp.dma_start(const[:, :], consts).then_inc(const_in, 16)
            sp.dma_start(gsm[:, :, :], gates).then_inc(gate_in, 16)
            sp.dma_start(la_nat, lora_a.rearrange("(t n) r l -> (n r) t l", n=4)).then_inc(lora_in, 16)
            sp.dma_start(lbT, lora_bT).then_inc(lora_in, 16)
            sp.dma_start(aT[:, :, G, :], lora_asT).then_inc(lora_in, 16)
            for i in range(2):
                sp.dma_start(bT[32:64, i, :], lora_bsT).then_inc(lora_in, 16)
            sp.dma_start(wqkvT[:, :, :], w_qkvT).then_inc(wqkv_in, 16)
            sp.dma_start(bqk[:, :], bqk_d).then_inc(wide_in, 16)
            sp.dma_start(bv_row, b_qkv[2 * L:3 * L].partition_broadcast(128)).then_inc(wide_in, 16)
            sp.dma_start(bo_row, b_out.partition_broadcast(128)).then_inc(wide_in, 16)
            sp.dma_start(bf_row, ffn_b.partition_broadcast(128)).then_inc(wide_in, 16)
            sp.wait_ge(style_ready, 1)
            sp.dma_start(chs[:, :], chain_s[1]).then_inc(chs_in[1], 16)
            for g in range(HG, G):
                sp.wait_ge(acc_ready, first_use[("L2", 0, g - HG)] + 2)
                first_input(g)
            for g in range(G):
                sp.dma_start(xres[:, g, :], x[GB * g:GB * g + GB].rearrange("b c l -> (b c) l")).then_inc(x_in[g], 16)
            sp.dma_start(woT[:, :, :], w_outT).then_inc(wo_in, 16)
            for g in range(G):
                sp.wait_ge(xs_ready, g + 1)
                sp.dma_start(scratch[g], xs[:, g % 2]).then_inc(xs_out[g % 2], 16)
                sp.wait_ge(xs_out[g % 2], 16 * (g // 2 + 1))
                before = nth(1, g) - HG - 1
                sp.wait_ge(acc_ready, first_use[("L2", before // G, before % G)] + 2)
                for p in range(PH):
                    sp.dma_start(xp[32 * p:32 * p + 32, g % HG, :, 1:1 + M],
                                 scratch[g, :, p, :].rearrange("(b c) m -> c b m", b=GB)).then_inc(xp_in[g % HG], 16)
                if g == HG - 1:
                    sp.wait_ge(ct_ready, G)
                    sp.dma_start(chw[:, :], chain_w[1]).then_inc(chw_in[1], 16)
                    sp.wait_ge(acc_ready, first_use[("QKV", 0, G - 1)] + 3)
                    sp.dma_start(kff, ffn_w.rearrange("(m s) o -> m s o", s=PH)).then_inc(kff_in, 16)
            for g in range(G):
                sp.wait_ge(y_ready, g + 1)
                sp.dma_start(out[GB * g:GB * g + GB].rearrange("b c l -> (b c) l"), yout[:, g % 2, :]).then_inc(y_out[g % 2], 16)
            for i in range(2):
                sp.wait_ge(y_out[i], 16 * (G // 2))

        @block.tensor
        def _(pe):
            mm = nc.tensor.matmul

            def project_style(step, c):
                a = take(pe, step)
                pe.wait_ge(chs_in[c], 16)
                for l in range(NL):
                    last = mm(a[:, B * l:B * l + B], mwT[:, l, :], styT, start=True, stop=True)
                last.then_inc(acc_ready, 1)

            def sum_squares(step, c):
                a = take(pe, step)
                pe.wait_ge(sq_ready, c + 1)
                for l in range(NL):
                    last = mm(a[:, B * l:B * l + B], w2sum[:, l].rearrange("p a b -> p (a b)"), sq[:, l, :],
                              start=True, stop=True)
                last.then_inc(acc_ready, 1)

            def demod_rows(step, c):
                pe.wait_ge(diag_ready, c + 1)
                if c == 0:
                    pe.wait_ge(zeros, 2)
                for i in range(2):
                    a = take(pe, step, i)
                    mm(a, scale32[:, :], d4diag[:, 16 * i:16 * i + 16, :].rearrange("p a b -> p (a b)"),
                       start=True, stop=True).then_inc(acc_ready, 1)

            def layer1(step, c, g):
                a = [take(pe, step, 0), take(pe, step, 1)]
                for i in range(2):
                    if c == 0:
                        pe.wait_ge(x_scaled, g + i + 1)
                    else:
                        pe.wait_ge(xp_in[(g + i) % HG], 16 * 2 + 64 * ((g + i) // HG + 1))
                    mm(a[i], t1[:], xp[:, (g + i) % HG, :, 1:1 + M], start=True, stop=False, skip_group_check=True)
                def before(i):
                    return mm(a[i][0:32, :], wT[96:128, 2, 0, :], xp[96:128, (g + i) % HG, :, 0:M], start=False,
                              stop=False, tile_position=(96, 0), skip_group_check=True)

                def after(i):
                    return mm(a[i][96:128, :], wT[0:32, 0, 0, :], xp[0:32, (g + i) % HG, :, 2:2 + M], start=False,
                              stop=True, tile_position=(0, 96), skip_group_check=True)

                before(0)
                after(1)
                after(0)
                before(1).then_inc(acc_ready, 2)

            def layer2(step, c, g):
                a, b = take(pe, step, 0), take(pe, step, 1)
                pe.wait_ge(z1_ready, nth(c, g))
                src = z1[:, g % HG]
                mm(a, t2[:, 0].rearrange("p a b -> p (a b)"), src[:, :, 1:1 + M], start=True, stop=False, skip_group_check=True)
                mm(b, t2[:, 1].rearrange("p a b -> p (a b)"), src[:, :, 1:1 + M], start=True, stop=False, skip_group_check=True)
                mm(a[0:64, :], taps2[96:128, 4:6, :].rearrange("p a b -> p (a b)"), src[96:128, :, 0:M], start=False, stop=True,
                   tile_position=(96, 0), skip_group_check=True).then_inc(acc_ready, 1)
                mm(b[64:128, :], taps2[0:32, 0:2, :].rearrange("p a b -> p (a b)"), src[0:32, :, 2:2 + M], start=False, stop=True,
                   tile_position=(0, 64), skip_group_check=True).then_inc(acc_ready, 1)

            def layer3(step, c, g):
                a, b = take(pe, step, 0), take(pe, step, 1)
                pe.wait_ge(z2_fixed, nth(c, g))
                sa, sb_ = z2[:, 0, g % 2], z2[:, 1, g % 2]
                w = t3[:]
                mm(a, w, sa[:, :, 1:1 + M], start=True, stop=False, skip_group_check=True)
                mm(b, w, sb_[:, :, 1:1 + M], start=True, stop=False, skip_group_check=True)
                before, after = wT[96:128, 2, 2, :], wT[0:32, 0, 2, :]
                mm(a[0:32, :], before, sb_[96:128, :, 0:M], start=False, stop=False, tile_position=(96, 0), skip_group_check=True)
                mm(b[96:128, :], after, sa[0:32, :, 2:2 + M], start=False, stop=False, tile_position=(0, 96), skip_group_check=True)
                mm(a[96:128, :], after, sb_[0:32, :, 1:1 + M], start=False, stop=True, tile_position=(0, 96), skip_group_check=True)
                mm(b[0:32, :], before, sa[96:128, :, 1:1 + M], start=False, stop=True, tile_position=(96, 0),
                   skip_group_check=True).then_inc(acc_ready, 2)

            def layer4(step, c, g):
                a = take(pe, step)
                pe.wait_ge(halo_ready, nth(c, g))
                for b in range(GB):
                    o = a[:, 128 * b:128 * b + 128]
                    for i, z in enumerate((z3[:, 0, g % 2, b, 1:1 + M], z3[:, 1, g % 2, b, 1:1 + M], halo[:, g % 2, b, :])):
                        last = mm(o, z, t4[:, i].rearrange("p a b -> p (a b)"), start=i == 0, stop=i == 2)
                last.then_inc(acc_ready, 1)

            def lora(step):
                pe.wait_ge(lora_in, 16 * 5)
                pe.wait_ge(lprep, 1)
                for i in range(2):
                    a = take(pe, step, i)
                    for half in range(2):
                        s = 2 * i + half
                        for t in range(4):
                            lhs = la_nat[:, t, :].rearrange("p (m s) -> p s m", s=PH)[:, s, :]
                            last = mm(a[:, 256 * half:256 * half + 256], lhs, gmat[:, t].rearrange("p g r -> p (g r)"),
                                      start=t == 0, stop=t == 3)
                    last.then_inc(acc_ready, 1)
                for h in range(2):
                    a = take(pe, step, 2 + h)
                    for t in range(4):
                        last = mm(a, gmat[:, t, 4 * h:4 * h + 4, :].rearrange("p g r -> p (g r)"), lbT[:, t, :], start=t == 0, stop=t == 3)
                    last.then_inc(acc_ready, 1)

            def qkv(step, g):
                if g == 0:
                    pe.wait_ge(wqkv_in, 16)
                pe.wait_ge(ct_ready, nth(0, g))
                src = cT[:, g % HG]
                for i in range(2):
                    a = take(pe, step, i)
                    for t in range(NT):
                        for s in range(PH):
                            col = (NT * i + t) * 128
                            last = mm(a[:, 128 * t:128 * t + 128], wqkvT[:, s, col:col + 128], src[:, s, :], start=s == 0, stop=s == 3)
                    last.then_inc(acc_ready, 1)
                a = take(pe, step, 2)
                for s in range(PH):
                    last = mm(a, src[:, s, :], wqkvT[:, s, 2 * L:3 * L], start=s == 0, stop=s == 3)
                last.then_inc(acc_ready, 1)

            def scores(step, g):
                a = [take(pe, step, 0), take(pe, step, 1)]
                pe.wait_ge(q_ready, g + 1)
                for t in range(NT):
                    pe.wait_ge(km_ready[t], g + 1)
                    for b in range(GB):
                        last = mm(a[t // 2][32 * b:32 * b + 32, 256 * (t % 2):256 * (t % 2) + 256],
                                  qT[:, g % 2, t, 32 * b:32 * b + 32], km[:, t, :, 32 * b:32 * b + 32],
                                  start=True, stop=True, tile_position=(0, 32 * b))
                    if t % 2:
                        last.then_inc(acc_ready, 1)

            def values(step, g):
                a = take(pe, step)
                for r2 in range(2):
                    pe.wait_ge(pblk_ready, 2 * g + r2 + 1)
                    for t in (2 * r2, 2 * r2 + 1):
                        for e in range(2):
                            for j in range(4):
                                col = (8 * t + 2 * j) * HD
                                last = mm(a[32 * j:32 * j + 32, 128 * t:128 * t + 128], v2[:, g % HG, e, col:col + 32],
                                          pblk[:, r2, 8 * (t % 2) + 2 * j + e, :], start=e == 0, stop=e == 1,
                                          tile_position=(0, 32 * j))
                    if r2 == 0:
                        last.then_inc(pv_half, 1)
                last.then_inc(acc_ready, 1)

            def output(step, g):
                a = take(pe, step)
                if g == 0:
                    pe.wait_ge(wo_in, 16)
                pe.wait_ge(oT_ready, g + 1)
                for t in range(NT):
                    last = mm(a, oT[:, g % 2, 128 * t:128 * t + 128], woT[:, t, :], start=t == 0, stop=t == NT - 1)
                last.then_inc(acc_ready, 1)

            def low_rank(step, g):
                a = take(pe, step)
                if g == 0:
                    pe.wait_ge(lprep, 5)
                pe.wait_ge(ct_ready, nth(1, g))
                for s in range(PH):
                    for i, gi in enumerate((g, G)):
                        last = mm(a[32 * i:32 * i + 32, 0:128], aT[:, s, gi, :], cT[:, g % HG, s, :], start=s == 0, stop=s == 3,
                                  tile_position=(0, 32 * i))
                last.then_inc(acc_ready, 1)

            def feed_forward(step, g):
                a = take(pe, step)
                if g == 0:
                    pe.wait_ge(kff_in, 16)
                for s in range(PH):
                    mm(a, cT[:, g % HG, s, :], kff[:, s, :], start=s == 0, stop=False)
                pe.wait_ge(ax_ready, g + 1)
                pe.wait_ge(bt_ready, g + 1)
                mm(a, axT[:, g % 2, :], bT[:, g % 2, :], start=False, stop=True).then_inc(acc_ready, 1)

            for step in order:
                kind, c, g = step
                if kind == "PA":
                    project_style(step, c)
                elif kind == "PB":
                    sum_squares(step, c)
                elif kind == "PC":
                    demod_rows(step, c)
                elif kind == "L1":
                    if g == 0:
                        pe.wait_ge(chw_in[c], 16)
                        pe.wait_ge(zeros, 1)
                    layer1(step, c, g)
                elif kind == "L2":
                    if g == 0:
                        pe.wait_ge(t2_ready, c + 1)
                    layer2(step, c, g)
                elif kind == "L3":
                    layer3(step, c, g)
                elif kind == "L4":
                    if g == 0:
                        pe.wait_ge(t4_ready, c + 1)
                    layer4(step, c, g)
                elif kind == "LORA":
                    lora(step)
                elif kind == "QKV":
                    qkv(step, g)
                elif kind == "SC":
                    scores(step, g)
                elif kind == "PV":
                    values(step, g)
                elif kind == "OUT":
                    output(step, g)
                elif kind == "AX":
                    low_rank(step, g)
                else:
                    feed_forward(step, g)

        @block.scalar
        def _(act):
            def scaled(dst, step, i, c, g, layer, tile_rows=None):
                a = filled(act, step, i)
                for b in range(GB):
                    at = GB * g + b
                    last = nc.scalar.activation(dst[:, b, 1:1 + M], a[:, M * b:M * b + M], ACT.Identity,
                                                bias=tabB[:, layer, at:at + 1], scale=tabA[:, layer, at:at + 1])
                return last

            def exponentials(g):
                act.wait_ge(shifted, g + 1)
                nc.scalar.activation(S[:, g % HG, :], S[:, g % HG, :], ACT.Exp).then_inc(exp_done, 1)

            for n, step in enumerate(order):
                kind, c, g = step
                if kind == "PB":
                    act.wait_ge(var_read, c + 1)
                    nc.scalar.activation(dv[:, 1].rearrange("p a b -> p (a b)"), dv[:, 0].rearrange("p a b -> p (a b)"),
                                         ACT.Sqrt).then_inc(sqrt_ready, 1)
                elif kind == "L1":
                    if g == 0:
                        act.wait_ge(tab_ready, c + 1)
                    for i in range(2):
                        scaled(z1[:, (g + i) % HG], step, i, c, g + i, 0).then_inc(z1_ready, 1)
                elif kind == "L2":
                    for i in range(2):
                        scaled(z2[:, i, g % 2], step, i, c, g, 1).then_inc(z2_ready, 1)
                elif kind == "L3":
                    for i in range(2):
                        scaled(z3[:, i, g % 2], step, i, c, g, 2).then_inc(z3_ready, 1)
                elif kind == "PV":
                    a = filled(act, step)
                    nc.scalar.activation(oT[:, g % 2, :], a, ACT.Copy).then_inc(oT_ready, 1)
                elif kind == "AX":
                    a = filled(act, step)
                    nc.scalar.activation(axT[:, g % 2, :], a[0:64, 0:128], ACT.Copy).then_inc(ax_ready, 1)
                    if g >= 2:
                        act.wait_ge(acc_ready, first_use[("Y", 1, g - 2)] + 1)
                    if g == 0:
                        act.wait_ge(lprep, 5)
                    q = 32 * (g % 4)
                    nc.scalar.activation(bT[0:32, g % 2, :], bT4[q:q + 32, g // 4, :], ACT.Copy).then_inc(bt_ready, 1)
                for g2 in exp_after.get(n, []):
                    exponentials(g2)

        @block.gpsimd
        def _(pool):
            tt = nc.gpsimd.tensor_tensor
            steps = [0]

            def after(ins):
                steps[0] += 1
                ins.then_inc(pool_done, 1)
                pool.wait_ge(pool_done, steps[0])

            for pad in (0, MP - 1):
                nc.gpsimd.memset(xp[:, :, :, pad], 0.0)
                for z in (z2, z3):
                    for i in range(2):
                        last = nc.gpsimd.memset(z[:, i, :, :, pad], 0.0)
            last.then_inc(zeros, 1)
            pool.wait_ge(zeros, 1)
            nc.gpsimd.memset(t2[:, :, :, :], 0.0)
            nc.gpsimd.memset(t4[:, :, :, :], 0.0)
            nc.gpsimd.memset(scale32[:, :], SCALE).then_inc(zeros, 1)
            pool.wait_ge(zeros, 2)
            nc.gpsimd.memset(pblk[:, :, :, :].rearrange("p a b c -> p (a b c)"), 0.0).then_inc(cleared, 1)
            pool.wait_ge(cleared, 1)
            for step in order:
                kind, c, g = step
                if kind == "PB":
                    pool.wait_ge(taps_ready, 2 * c + 1)
                    for p in range(PH):
                        q = slice(32 * p, 32 * p + 32)
                        lo, hi = max(0, 2 * p - 2), min(8, 2 * p + 4)
                        tile = nc.gpsimd.tensor_copy(t2[q].rearrange("p t n i -> p (t n) i")[:, lo:hi, :],
                                                     taps2[q, lo - 2 * p + 2:hi - 2 * p + 2, :])
                        if p < PH - 1:
                            after(tile)
                    tile.then_inc(t2_ready, 1)
                    pool.wait_ge(t2_ready, c + 1)
                elif kind == "PC":
                    pool.wait_ge(taps_ready, 2 * c + 2)
                    for p in range(PH):
                        q = slice(32 * p, 32 * p + 32)
                        for i, n in enumerate((p, p + 4, p + 8 if p < 2 else p - 4)):
                            ss = [s for s in range(PH) if 0 <= 3 - n + 2 * s <= 5]
                            r0 = 3 - n + 2 * ss[0]
                            tile = nc.gpsimd.tensor_copy(t4[q, i, ss[0]:ss[-1] + 1, :],
                                                         taps4[q, r0:r0 + 2 * len(ss) - 1:2, :])
                            if (p, i) < (PH - 1, 2):
                                after(tile)
                    tile.then_inc(t4_ready, 1)
                    pool.wait_ge(t4_ready, c + 1)
                elif kind == "LORA":
                    pool.wait_ge(acc_ready, first_use[step] + 4)
                    nc.gpsimd.memset(v2f, 0.0).then_inc(cleared, 1)
                    pool.wait_ge(cleared, 2)
                elif kind == "L2":
                    pool.wait_ge(z2_ready, 2 * nth(c, g))
                    at = slice(GB * g, GB * g + GB)
                    first, last = z2[0:32, 0, g % 2, :, 1], z2[96:128, 1, g % 2, :, M]
                    after(tt(first, first, edge[0:32, at], ALU.subtract))
                    tt(last, last, edge[96:128, at], ALU.subtract).then_inc(z2_fixed, 1)
                    pool.wait_ge(z2_fixed, nth(c, g))
                elif kind == "L3":
                    if nth(c, g) > 2:
                        before = nth(c, g) - 3
                        pool.wait_ge(acc_ready, first_use[("L4", before // G, before % G)] + 1)
                    pool.wait_ge(z3_ready, 2 * nth(c, g))
                    after(nc.gpsimd.tensor_copy(halo[0:64, g % 2], z3[0:64, 0, g % 2, :, 2:2 + M]))
                    nc.gpsimd.tensor_copy(halo[64:128, g % 2], z3[64:128, 1, g % 2, :, 0:M]).then_inc(halo_ready, 1)
                    pool.wait_ge(halo_ready, nth(c, g))
                elif kind == "QKV":
                    pool.wait_ge(k_ready, g + 1)
                    if g >= 1:
                        pool.wait_ge(acc_ready, first_use[("SC", 0, g - 1)] + 2)
                    mask = const[:, C_MASK:C_MASK + 8].unsqueeze(2).broadcast_to((128, 8, 128))
                    for t in range(NT):
                        tt(km[:, t], kT[:, g % 2, t, :].unsqueeze(1).broadcast_to((128, 8, 128)), mask,
                           ALU.mult).then_inc(km_ready[t], 1)
                        pool.wait_ge(km_ready[t], g + 1)
                elif kind == "OUT":
                    pool.wait_ge(xs_ready, g + 1)
                    tt(xres[:, g, :], xres[:, g, :], bf_row, ALU.add).then_inc(xf_ready, 1)
                    pool.wait_ge(xf_ready, g + 1)

        @block.vector
        def _(dve):
            v = nc.vector
            tt, stt, ts, copy = v.tensor_tensor, v.scalar_tensor_tensor, v.tensor_scalar, v.tensor_copy
            links = [0]

            def link(ins):
                links[0] += 1
                ins.then_inc(dve_done, 1)
                dve.wait_ge(dve_done, links[0])

            def scale_first(g):
                dve.wait_ge(xp_in[g % HG], 16 * (g // HG + 1))
                part = xp[:, g % HG, :, 1:1 + M]
                tt(part, part, stab2[:, 0, 0, GB * g:GB * g + GB].unsqueeze(2).broadcast_to((128, GB, M)), ALU.mult).then_inc(x_scaled, 1)

            def scale_second(g):
                if g >= 2:
                    dve.wait_ge(xs_out[g % 2], 16 * (g // 2))
                ts(xs[:, g % 2], xres[:, g, :].rearrange("p (m s) -> p s m", s=PH), sin[:, g:g + 1], None,
                   ALU.mult).then_inc(xs_ready, 1)

            def style_scales(step, c):
                a = filled(dve, step)
                tt(stab2[:, c], a[:, 0:NL * B].rearrange("p (l b) -> p l b", l=NL),
                   mbr.unsqueeze(2).broadcast_to((128, NL, B)), ALU.add).then_inc(style_ready, 1)
                dve.wait_ge(style_ready, c + 1)
                if c == 0:
                    scale_first(0)
                    scale_first(1)
                else:
                    for j in range(GB):
                        last = copy(sin[32 * j:32 * j + 32, :], stab2[32 * j:32 * j + 32, 1, 0, :].rearrange("p (g j) -> p j g", j=GB)[:, j, :])
                    link(last)

            def squares(c):
                dve.wait_ge(chw_in[c], 16)
                tt(sq[:, :, :], stab2[0:32, c], stab2[0:32, c], ALU.mult)
                wt = [wT[0:32, k] for k in range(TAPS)]
                link(tt(w2sq[:, 0], wt[0], wt[0], ALU.mult))
                link(tt(w2sq[:, 1], wt[1], wt[1], ALU.mult))
                link(tt(w2sq[:, 0], w2sq[:, 0], w2sq[:, 1], ALU.add))
                link(tt(w2sq[:, 1], wt[2], wt[2], ALU.mult))
                link(tt(w2sq[:, 0], w2sq[:, 0], w2sq[:, 1], ALU.add))
                copy(w2sum[:, :, :, :], w2sq[:, 0].unsqueeze(2).broadcast_to((32, NL, PH, C))).then_inc(sq_ready, 1)

            def tables(step, c):
                stab = stab2[:, c]
                v.memset(taps4[:, :, :], 0.0)
                link(v.memset(taps2[:, :, :], 0.0))
                for j in range(4):
                    dst = taps2[:, 3 - j:6 - j, :]
                    tap = stt(dst, w_up[:], 2.0 * BLUR[j], dst, ALU.mult, ALU.add)
                    if j < 3:
                        link(tap)
                tap.then_inc(taps_ready, 1)
                a = filled(dve, step)
                flat = [dv[:, i].rearrange("p a b -> p (a b)") for i in range(3)]
                ts(flat[0], a[:, 0:NL * B], SCALE * SCALE, EPS, ALU.mult, ALU.add).then_inc(var_read, 1)
                dve.wait_ge(var_read, c + 1)
                d = dd[:, :, :].rearrange("p a b -> p (a b)")
                dve.wait_ge(sqrt_ready, c + 1)
                link(v.reciprocal(flat[1], flat[1]))
                link(tt(flat[2], flat[1], flat[1], ALU.mult))
                link(tt(flat[2], flat[2], flat[0], ALU.mult))
                link(ts(flat[2], flat[2], -0.5, 1.5, ALU.mult, ALU.add))
                link(tt(d, flat[1], flat[2], ALU.mult))
                b = [cbr[:, l:l + 1] for l in range(NL)]
                stt(tabA[:, 0, :], dd[:, 0, :], SCALE, dd[:, 1, :], ALU.mult, ALU.mult)
                ts(tabB[:, 0, :], dd[:, 1, :], b[0], None, ALU.mult)
                stt(tabA[:, 1, :], stab[:, 1, :], SCALE, stab[:, 2, :], ALU.mult, ALU.mult)
                ts(tabB[:, 1, :], stab[:, 2, :], b[1], 2.0, ALU.mult, ALU.mult)
                ts(edge[:, :], stab[:, 2, :], b[1], 2.0 * BLUR_EDGE, ALU.mult, ALU.mult)
                stt(tabA[:, 2, :], dd[:, 2, :], SCALE, stab[:, 3, :], ALU.mult, ALU.mult)
                ts(tabB[:, 2, :], stab[:, 3, :], b[2], None, ALU.mult).then_inc(tab_ready, 1)
                if c == 0:
                    dve.wait_ge(const_in, 16)
                if c == 1:
                    for i in range(2):
                        dve.wait_ge(xs_out[i], 32)
                tt(d4diag[:, :, :], dd[0:32, 3, :].unsqueeze(2).broadcast_to((32, B, C)),
                   const[0:32, C_SEL:C_SEL + C].unsqueeze(1).broadcast_to((32, B, C)), ALU.mult).then_inc(diag_ready, 1)
                if c == 0:
                    scale_first(2)
                    scale_first(3)
                for j in range(4):
                    dst = taps4[:, 3 - j:6 - j, :]
                    tap = stt(dst, wT[:, :, 3, :], BLUR[j], dst, ALU.mult, ALU.add)
                    if j < 3:
                        link(tap)
                tap.then_inc(taps_ready, 1)

            def scale_rows(step, c):
                for i in range(2):
                    a = filled(dve, step, i)
                    last = copy(d4row[:, 16 * i:16 * i + 16, :].rearrange("p b o -> p (b o)"), a)
                last.then_inc(d4_ready, 1)

            def lora(step):
                dve.wait_ge(gate_in, 16)
                sel = const[:, C_SEL:C_SEL + C].unsqueeze(1).broadcast_to((128, G, RANK))
                for t in range(4):
                    last = tt(gmat[:, t], gsm[:, t, :].unsqueeze(2).broadcast_to((128, G, RANK)), sel, ALU.mult)
                last.then_inc(lprep, 1)
                for i in range(2):
                    a = filled(dve, step, i)
                    copy(aT[:, 2 * i:2 * i + 2, 0:G, :], a.rearrange("p (s g r) -> p s g r", s=2, g=G)).then_inc(lprep, 1)
                for h in range(2):
                    a = filled(dve, step, 2 + h)
                    copy(bT4[:, h, :], a).then_inc(lprep, 1)

            def down_out(step, c, g):
                a = filled(dve, step)
                view = cT[:, g % HG].rearrange("p s (b o) -> p b s o", b=GB)
                for b in range(GB):
                    last = tt(view[:, b], a[:, 128 * b:128 * b + 128].rearrange("p (s o) -> p s o", s=PH),
                              d4row[:, GB * g + b, :].unsqueeze(1).broadcast_to((128, PH, C)), ALU.mult)
                link(last)
                flat = cT[:, g % HG].rearrange("p s (b o) -> p (s b) o", b=GB)
                tt(flat, flat, b4row[:, :].unsqueeze(1).broadcast_to((128, PH * GB, C)), ALU.add).then_inc(ct_ready, 1)

            def qkv(step, g):
                if g == 0:
                    dve.wait_ge(wide_in, 64)
                    dve.wait_ge(cleared, 2)
                for i, (dst, ready) in enumerate(((qT, q_ready), (kT, k_ready))):
                    a = filled(dve, step, i)
                    tt(dst[:, g % 2], a.rearrange("p (t n) -> p t n", t=NT),
                       bqk[:, NT * i:NT * i + NT].unsqueeze(2).broadcast_to((128, NT, 128)), ALU.add).then_inc(ready, 1)
                a = filled(dve, step, 2)
                for e in range(2):
                    pick = lambda ap: ap.rearrange("p (n e d) -> p e n d", e=2, d=HD)[:, e]
                    last = tt(pick(v2[:, g % HG, e, :]), pick(a), pick(bv_row), ALU.add)
                last.then_inc(v_ready, 1)

            def scores(step, g):
                for i in range(2):
                    a = filled(dve, step, i)
                    half = slice(512 * i, 512 * i + 512)
                    stt(S[:, g % HG, half], a, QK_SCALE, const[:, C_ALIBI + 512 * i:C_ALIBI + 512 * i + 512], ALU.mult,
                        ALU.add).then_inc(scored, 1)
                dve.wait_ge(scored, 2 * g + 2)
                rows_ = S[:, g % HG, :].rearrange("p (h k) -> p h k", k=C)
                link(v.tensor_reduce(stat[:, 0, g % HG, :], rows_, AX_X, ALU.max))
                tt(rows_, rows_, stat[:, 0, g % HG, :].unsqueeze(2).broadcast_to((128, HEADS, C)), ALU.subtract).then_inc(shifted, 1)

            def normalise(g):
                dve.wait_ge(exp_done, g + 1)
                rows_ = S[:, g % HG, :].rearrange("p (h k) -> p h k", k=C)
                link(v.tensor_reduce(stat[:, 1, g % HG, :], rows_, AX_X, ALU.add))
                link(v.reciprocal(stat[:, 1, g % HG, :], stat[:, 1, g % HG, :]))
                link(tt(rows_, rows_, stat[:, 1, g % HG, :].unsqueeze(2).broadcast_to((128, HEADS, C)), ALU.mult))

            def turn(g):
                for r2 in range(2):
                    if g >= 1:
                        if r2 == 0:
                            dve.wait_ge(pv_half, g)
                        else:
                            dve.wait_ge(acc_ready, first_use[("PV", 0, g - 1)] + 1)
                    for b in range(GB):
                        q = slice(32 * b, 32 * b + 32)
                        last = v.transpose(pblk[q, r2, :, 32 * b:32 * b + 32],
                                           S[q, g % HG, 512 * r2:512 * r2 + 512].rearrange("p (h k) -> p h k", k=C))
                    last.then_inc(pblk_ready, 1)

            def residual(step, g):
                a = filled(dve, step)
                dve.wait_ge(x_in[g], 16)
                tt(xres[:, g, :], xres[:, g, :], a, ALU.add).then_inc(added, 1)
                dve.wait_ge(added, g + 1)
                link(tt(xres[:, g, :], xres[:, g, :], bo_row, ALU.add))
                scale_second(g)

            def last_sum(step, g):
                a = filled(dve, step)
                dve.wait_ge(xf_ready, g + 1)
                if g >= 2:
                    dve.wait_ge(y_out[g % 2], 16 * (g // 2))
                else:
                    dve.wait_ge(xs_out[g], 16 * (G // 2))
                tt(yout[:, g % 2, :], a, xres[:, g, :], ALU.add).then_inc(y_ready, 1)

            for n, step in enumerate(order):
                kind, c, g = step
                if kind == "PA":
                    style_scales(step, c)
                elif kind == "PB":
                    squares(c)
                    tables(step, c)
                elif kind == "PC":
                    scale_rows(step, c)
                elif kind == "LORA":
                    lora(step)
                elif kind == "L4":
                    down_out(step, c, g)
                elif kind == "QKV":
                    qkv(step, g)
                    if g < HG:
                        scale_first(HG + g)
                elif kind == "SC":
                    scores(step, g)
                elif kind == "OUT":
                    residual(step, g)
                elif kind == "PV" and g % HG < 3:
                    turn(g + 1)
                elif kind == "Y":
                    last_sum(step, g)
                for g2 in norm_after.get(n, []):
                    normalise(g2)
                    if g2 % HG == 3:
                        turn(g2 - 3)


_INS = ["x", "cond_512"] + [f"L0_{c}_{n}" for c in ("cond", "cond2") for n in ("weights", "biases", "mod_w", "mod_b")] + [
    "L0_attn_w_qkv", "L0_attn_b_qkv", "L0_attn_w_out", "L0_attn_b_out", "L0_ffn_gate", "L0_ffn_kernel", "L0_ffn_bias",
    "L0_ffn_lora_A", "L0_ffn_lora_B", "L0_ffn_lora_A_shared", "L0_ffn_lora_B_shared"]


def kernel(**inputs):
    import concourse.bacc as bacc
    from concourse.bass_utils import run_bass_kernel_spmd

    nc = bacc.Bacc("TRN2", target_bir_lowering=False, num_devices=1)
    v = {n: np.ascontiguousarray(inputs[n]) for n in _INS}
    attn, ffn = "L0_attn_", "L0_ffn_"
    arrays = {
        "x": v["x"],
        "xph": v["x"].reshape(G, GB, C, M, PH).transpose(0, 4, 2, 1, 3).reshape(G, 128, GB, M),
        "w_qkvT": v[attn + "w_qkv"].T.reshape(M, PH, NQKV * 128),
        "bqk": v[attn + "b_qkv"][:2 * L].reshape(2 * NT, 128).T,
        "b_qkv": v[attn + "b_qkv"],
        "w_outT": v[attn + "w_out"].T.reshape(NT, 128, L).transpose(1, 0, 2),
        "b_out": v[attn + "b_out"],
        "gates": np.repeat(v[ffn + "gate"].T.reshape(4, 4, G).transpose(1, 0, 2), RANK, axis=0),
        "ffn_w": v[ffn + "kernel"],
        "ffn_b": v[ffn + "bias"],
        "lora_a": v[ffn + "lora_A"],
        "lora_bT": v[ffn + "lora_B"].transpose(0, 2, 1).reshape(4, 4 * RANK, L).transpose(1, 0, 2),
        "lora_asT": v[ffn + "lora_A_shared"].T.reshape(M, PH, RANK),
        "lora_bsT": v[ffn + "lora_B_shared"].T,
        "consts": shape_constants(),
    }
    for i, c in enumerate(("cond", "cond2")):
        arrays[f"chain_w{i}"], arrays[f"chain_s{i}"] = pack_chain(
            *(v[f"L0_{c}_{n}"] for n in ("weights", "biases", "mod_w", "mod_b")), v["cond_512"])
    arrays = {n: np.ascontiguousarray(a) for n, a in arrays.items()}
    d = {n: nc.dram_tensor("in_" + n, a.shape, mybir.dt.from_np(a.dtype), kind="ExternalInput").ap() for n, a in arrays.items()}
    out = nc.dram_tensor("out", (B, C, L), F32, kind="ExternalOutput").ap()
    build(nc, d["x"], d["xph"], [d["chain_w0"], d["chain_w1"]], [d["chain_s0"], d["chain_s1"]], d["w_qkvT"], d["bqk"],
          d["b_qkv"], d["w_outT"], d["b_out"], d["gates"], d["ffn_w"], d["ffn_b"], d["lora_a"], d["lora_bT"],
          d["lora_asT"], d["lora_bsT"], d["consts"], out)
    arrays = {"in_" + n: a for n, a in arrays.items()}
    r = run_bass_kernel_spmd(nc, [arrays], core_ids=[0])
    return r.results[0]["out"]
```

```python
from contextlib import ExitStack

import numpy as np

import concourse.bass as bass
from concourse import mybir

F32 = mybir.dt.float32
F32R = mybir.dt.float32r
ALU = mybir.AluOpType
ACT = mybir.ActivationFunctionType
AX_X = mybir.AxisListType.X

B, C, L = 32, 32, 512
STYLE = 64
TAPS, PH = 3, 4
M = L // PH
MP = M + 2
G, GB = 8, 4
HG = G // 2
NL = 4
TILE_B = (5, 4, 7, 6)
HEADS, HD = 32, 16
NT = L // 128
NQKV = 3 * NT
RANK = 32
BANKS = 8
SCALE = 1.0 / float(np.sqrt(C * TAPS ** 2))
EPS = 1e-8
BLUR = [0.125, 0.375, 0.375, 0.125]
BLUR_EDGE = 0.125
QK_SCALE = 1.0 / float(np.sqrt(HD))

C_ALIBI, C_MASK = 0, HEADS * C
C_SEL = C_MASK + 8
N_CONST = C_SEL + C
W_T, W_UP, W_T1, W_T3 = 0, TAPS * NL * C, TAPS * NL * C + TAPS * C, TAPS * NL * C + TAPS * C + PH * C
W_T3B = W_T3 + PH * C
W_CB = W_T3B + PH * C
W_B4, N_W = W_CB + NL, W_CB + NL + C
S_T, S_MB, N_S = NL * PH * C, NL * PH * C + B, NL * PH * C + B + NL


def shape_constants():
    out = np.zeros((128, N_CONST), np.float32)
    slopes = (1.0 / 2.0 ** (np.arange(1, HEADS + 1, dtype=np.float32) * np.float32(8.0 / HEADS))).astype(np.float32)
    k, q = np.arange(C), np.arange(128) % C
    for h in range(HEADS):
        bias = slopes[h] * (k - (C - 1)).astype(np.float32)
        out[:, C_ALIBI + C * h:C_ALIBI + C * h + C] = np.where(q[:, None] >= k[None, :], bias[None, :], np.float32(-1e9))
    for c in range(8):
        out[:, C_MASK + c] = np.arange(128) // HD == c
    out[:, C_SEL:C_SEL + C] = np.tile(np.eye(C), (4, 1))
    return out


def pack_chain(w, b, mw, mb, style):
    out = np.zeros((128, N_W), np.float32)
    proj = np.zeros((128, N_S), np.float32)
    wt = w.transpose(2, 3, 0, 1)[:, ::-1]
    out[:, W_T:W_T + TAPS * NL * C] = np.tile(wt.reshape(C, -1), (PH, 1))
    out[:, W_UP:W_UP + TAPS * C] = np.tile(w[1].transpose(0, 2, 1).reshape(C, -1), (PH, 1))
    for at, l, phases in ((W_T1, 0, range(PH)), (W_T3, 2, range(PH)), (W_T3B, 2, TILE_B)):
        for i, p in enumerate(phases):
            for j, s in enumerate(phases):
                if abs(p - s) <= 1:
                    out[C * i:C * i + C, at + C * j:at + C * j + C] = w[l, :, :, p - s + 1].T
    out[:, W_CB:W_CB + NL] = np.tile(b.T, (PH, 1))
    out[:, W_B4:W_B4 + C] = b[3][None, :]
    proj[:STYLE, :S_T] = np.tile(mw.transpose(2, 0, 1)[:, :, None, :], (1, 1, PH, 1)).reshape(STYLE, -1)
    proj[:STYLE, S_T:S_MB] = style.T
    proj[:, S_MB:] = np.tile(mb.T, (PH, 1))
    return out, proj


def build(nc, x, xph, chain_w, chain_s, w_qkvT, bqk_d, b_qkv, w_outT, b_out, gates, ffn_w, ffn_b,
          lora_a, lora_bT, lora_asT, lora_bsT, consts, out):
    ctx = ExitStack()
    with ctx:
        def sb(name, shape, dtype=F32):
            return ctx.enter_context(nc.sbuf_tensor(name, shape, dtype))

        def sb_at(name, offset, shape, dtype=F32):
            return nc.alloc_sbuf_tensor_at(name, shape, dtype, offset=offset), offset + 4 * int(np.prod(shape[1:]))

        def sem(name):
            return ctx.enter_context(nc.semaphore(name))

        acc = ctx.enter_context(nc.psum_tensor("acc", [128, BANKS, 512], F32))
        const = sb("const", [128, N_CONST])
        xres = sb("xres", [128, G, L])
        xs = sb("xs", [128, 2, PH, M])
        xp = sb("xp", [128, 2, GB, MP])
        z1a = sb("z1a", [128, 2, GB, M + 1])
        z1b = sb("z1b", [128, 2, GB, M])
        z2 = sb("z2", [128, 2, 2, GB, MP])
        z3 = sb("z3", [128, 2, 2, GB, MP])
        halo = sb("halo", [128, 2, GB, M])
        ct_at = nc.sbuf_base
        cT = sb("cT", [128, HG, PH, 128])
        cL, _ = sb_at("cL", ct_at, [128, HG, PH, 128], F32R)
        ch_at = nc.sbuf_base
        cH = sb("cH", [128, HG, PH, 128], F32R)
        qt_at = nc.sbuf_base
        qT = sb("qT", [128, NT, 2, 128])
        kt_at = nc.sbuf_base
        kT = sb("kT", [128, NT, 2, 128])
        km_at = nc.sbuf_base
        km = sb("km", [128, NT, 8, 128])
        v2 = sb("v2", [128, 2, 2, L])
        S = sb("S", [128, 2, HEADS * C])
        pblk = sb("pblk", [128, 2, 16, 128])
        stat = sb("stat", [128, 2, 2, HEADS])
        oT = sb("oT", [128, 2, NT * 128])
        w_at = nc.sbuf_base
        wqkvT = sb("wqkvT", [128, PH, NQKV * 128])
        wL, _ = sb_at("wL", w_at, [128, PH, NQKV * 128], F32R)
        wh_at = nc.sbuf_base
        wH = sb("wH", [128, PH, NQKV * 128], F32R)
        woT = sb("woT", [128, NT, L])
        bqk = sb("bqk", [128, 2 * NT])
        rows = sb("rows", [128, 2, L])
        bv_row, bo_row = rows[:, 0, :], rows[:, 1, :]
        bf_row = bv_row
        chw = sb("chw", [128, N_W])
        chs = km[:, :, :, :].rearrange("p a b c -> p (a b c)")[:, 0:N_S]
        wT = chw[:, W_T:W_UP].rearrange("p (k l o) -> p k l o", k=TAPS, l=NL)
        w_up = chw[:, W_UP:W_T1].rearrange("p (k i) -> p k i", k=TAPS)
        t1, t3, t3b = chw[:, W_T1:W_T3], chw[:, W_T3:W_T3B], chw[:, W_T3B:W_CB]
        cbr, b4row = chw[:, W_CB:W_B4], chw[:, W_B4:N_W]
        mwT = chs[0:STYLE, 0:S_T].rearrange("p (l n) -> p l n", l=NL)
        styT, mbr = chs[0:STYLE, S_T:S_MB], chs[:, S_MB:N_S]
        stab2 = sb("stab", [128, 2, NL, B])
        taps2 = sb("taps2", [128, 6, C])
        taps4 = sb("taps4", [128, 6, C])
        t2 = sb("t2", [128, 2, PH, C])
        t4 = sb("t4", [128, 3, PH, C])
        sin = sb("sin", [128, G])
        tabA = sb("tabA", [128, 3, B])
        tabB = sb("tabB", [128, 3, B])
        edge = sb("edge", [128, B])
        scale32 = sb("scale32", [32, 128])
        d4row = sb("d4row", [128, B, C])
        gsm = sb("gsm", [128, NT, G])

        la_nat, at = sb_at("la_nat", km_at, [128, 4, L])
        lbT, _ = sb_at("lbT", at, [128, 4, L])
        gmat, _ = sb_at("gmat", qt_at, [128, 4, G, RANK])
        la = (sb_at("laH", w_at + 4 * 2 * PH * L, [128, 4, L], F32R)[0], sb_at("laL", km_at, [128, 4, L], F32R)[0])
        lb = (sb_at("lbH", ch_at, [128, 4, L], F32R)[0], sb_at("lbL", at, [128, 4, L], F32R)[0])
        gm = (sb_at("gmH", kt_at, [128, 4, G, RANK], F32R)[0], sb_at("gmL", qt_at, [128, 4, G, RANK], F32R)[0])

        kff, _ = sb_at("kff", w_at, [128, PH, L])
        kL, at = sb_at("kL", w_at, [128, PH, L], F32R)
        kH, at = sb_at("kH", at, [128, PH, L], F32R)
        aT, at = sb_at("aT", wh_at, [128, PH, G + 1, RANK])
        bT4, at = sb_at("bT4", at, [128, 2, L])
        bT, at = sb_at("bT", at, [128, 2, L])
        axT, at = sb_at("axT", at, [128, 2, 128])
        c2H, at = sb_at("c2H", at, [128, 2, PH * 128], F32R)
        c2L, at = sb_at("c2L", at, [128, 2, PH * 128], F32R)
        assert at <= wh_at + 4 * PH * NQKV * 128

        inside = z3[:, 0, :, :, 1:1 + M]
        dv = inside[:, 0, 0:3].rearrange("p n (l b) -> p n l b", l=NL)
        dd = inside[:, 0, 3].rearrange("p (l b) -> p l b", l=NL)
        sq = inside[0:32, 1, 0].rearrange("p (l b) -> p l b", l=NL)
        w2sum = z2[0:32, 0, 0, :, 1:1 + M].rearrange("p l (a i) -> p l a i", a=PH)
        w2sq, w2one = z2[0:32, 0, 1, 0:TAPS, 1:1 + M], z2[0:32, 0, 1, TAPS, 1:1 + M]
        d4diag = z2[0:32, 1, :, :, 1:1 + M]
        yout = xs[:, :, :, :].rearrange("p n s m -> p n (s m)")

        scratch = nc.dram_tensor("scratch", (G, 128, PH, M), F32, kind="Internal").ap()

        acc_ready = sem("acc_ready")
        const_in, x_in = sem("const_in"), [sem(f"x_in{i}") for i in range(G)]
        chs_in, chw_in = [sem(f"chs_in{i}") for i in range(2)], [sem(f"chw_in{i}") for i in range(2)]
        wide_in, wqkv_in, wo_in, kff_in, lora_in, gate_in = (
            sem(n) for n in ("wide_in", "wqkv_in", "wo_in", "kff_in", "lora_in", "gate_in"))
        zeros = sem("zeros")
        xs_ready = sem("xs_ready")
        xs_out = [sem(f"xs_out{i}") for i in range(2)]
        xp_in = [sem(f"xp_in{i}") for i in range(2)]
        x_scaled = sem("x_scaled")
        z1b_done, z1a_done, z1_ready = sem("z1b_done"), sem("z1a_done"), sem("z1_ready")
        z2_ready, z3_ready = [sem(f"z2_ready{i}") for i in range(2)], [sem(f"z3_ready{i}") for i in range(2)]
        z2_fixed = sem("z2_fixed")
        halo_ready = [sem(f"halo_ready{i}") for i in range(2)]
        ct_ready, q_ready, k_ready, v_ready = (sem(n) for n in ("ct_ready", "q_ready", "k_ready", "v_ready"))
        scored, added, pv_half, cleared = sem("scored"), sem("added"), sem("pv_half"), sem("cleared")
        km_ready = [sem(f"km_ready{t}") for t in range(NT)]
        shifted, exp_done, pblk_ready = sem("shifted"), sem("exp_done"), sem("pblk_ready")
        oT_ready, xf_ready = sem("oT_ready"), sem("xf_ready")
        ax_ready, bt_ready, y_ready = sem("ax_ready"), sem("bt_ready"), sem("y_ready")
        y_out = [sem(f"y_out{i}") for i in range(2)]
        dve_done, pool_done = sem("dve_done"), sem("pool_done")
        style_ready, sq_ready, var_read, diag_ready = (sem(n) for n in ("style_ready", "sq_ready", "var_read", "diag_ready"))
        sqrt_ready = sem("sqrt_ready")
        tab_ready, taps_ready, t2_ready, t4_ready, d4_ready = (
            sem(n) for n in ("tab_ready", "taps_ready", "t2_ready", "t4_ready", "d4_ready"))
        w_split, c_split, c2_split, k_split = (sem(n) for n in ("w_split", "c_split", "c2_split", "k_split"))
        bf_in = sem("bf_in")
        la_high, la_split, lb_high, lb_split = (sem(n) for n in ("la_high", "la_split", "lb_high", "lb_split"))
        w_high, w_low = sem("w_high"), sem("w_low")
        x_biased = sem("x_biased")
        lprep = sem("lprep")

        def of(c, names):
            steps = []
            for name in names.split():
                kind, g = name.split(".")
                steps.append((kind, c, int(g)))
            return steps

        order = of(0, "PA.0 PB.0 L1.0 PC.0 L2.0 L2.1 L1.2 L3.0 L2.2 L2.3 L4.0 L4.1 L3.2") + of(1, "PA.0")
        order += of(0, "L1.4 QK.0 V.0 V.1 L4.2 L2.4 L4.3 L2.5 SC.0 L1.6 L3.4 L2.6 SC.1")
        order += of(0, "QK.2 PV.0 V.2 L2.7 OUT.0 L4.4 SC.2 PV.1 V.3 L4.5 OUT.1 L3.6 SC.3")
        order += of(0, "QK.4 PV.2 V.4 L4.6 OUT.2 SC.4 PV.3 V.5 L4.7 OUT.3 SC.5")
        order += of(0, "QK.6") + of(1, "PB.0") + of(0, "PV.4 V.6 OUT.4") + of(1, "PC.0 L1.0") + of(0, "SC.6 PV.5")
        order += of(1, "L2.0") + of(0, "V.7") + of(1, "L2.1 L1.2") + of(0, "OUT.5") + of(1, "L3.0")
        order += of(0, "SC.7") + of(1, "L2.2 L2.3") + of(0, "PV.6") + of(1, "L4.0 L4.1") + of(0, "OUT.6") + of(1, "L3.2")
        order += of(0, "PV.7") + of(1, "LORA.0") + of(0, "OUT.7")
        order += of(1, "L4.2 LORA.1 L4.3 LORA.2 LORA.3 L1.4 AX.0 Y.0 AX.2 Y.1 L2.4 L2.5 L1.6 L3.4 L2.6 Y.2 L2.7 "
                       "L4.4 L4.5 Y.3 AX.4 L3.6 Y.4 L4.6 L4.7 Y.5 AX.6 Y.6 Y.7")
        banks_of = {"PA": 1, "PB": 1, "PC": 2, "L1": 2, "L2": 2, "L3": 4, "L4": 1, "LORA": 1, "QK": 4, "V": 1, "SC": 2, "PV": 1,
                    "OUT": 1, "AX": 1, "Y": 1}
        first_use, n = {}, 0
        for step in order:
            first_use[step] = n
            n += banks_of[step[0]]

        exp_after, norm_after, turn_after = {}, {}, {}
        for g in range(G):
            at = order.index(("SC", 0, g))
            exp_after[at + {7: 2}.get(g, 1)] = g
            later = at + {4: 3, 7: 4}.get(g, 4 - g % 2)
            norm_after[later] = g
            turn_after[max(later, order.index(("PV", 0, g - 1)) if g else 0)] = g
        assert len(exp_after) == len(norm_after) == len(turn_after) == G

        def bank(step, i=0):
            return acc[:, (first_use[step] + i) % BANKS, :]

        def take(pe, step, i=0):
            u = first_use[step] + i
            if u >= BANKS:
                reader, value = released[u - BANKS]
                pe.wait_ge(reader, value)
            return bank(step, i)

        def filled(eng, step, i=0):
            eng.wait_ge(acc_ready, first_use[step] + i + 1)
            return bank(step, i)

        def nth(c, g):
            return 8 * c + g + 1

        def by_dve(c, g):
            return c == 0 and g < HG or c == 1 and g >= 2

        def copied_by_act(c, g):
            return c == 1 and g < 2

        def z1_free(eng, c, g):
            before = nth(c, g) - 3
            if before >= 0:
                eng.wait_ge(acc_ready, first_use[("L2", before // G, before % G)] + 2)

        def halo_free(eng, c, g):
            before = nth(c, g) - 3
            if before >= 0:
                eng.wait_ge(acc_ready, first_use[("L4", before // G, before % G)] + 1)

        def acts_copies(c, g):
            return sum(copied_by_act(*divmod(n, G)) for n in range(nth(c, g)))

        def readers(step):
            kind, c, g = step
            return {
                "PA": lambda: [(style_ready, c + 1)],
                "PB": lambda: [(var_read, c + 1)],
                "PC": lambda: [(d4_ready, c + 1), (d4_ready, c + 1)],
                "L1": lambda: [(z1_ready, nth(c, g)), (z1_ready, nth(c, g + 1))],
                "L2": lambda: [(z2_ready[i], nth(c, g)) for i in range(2)],
                "L3": lambda: [(z3_ready[i % 2], nth(c, g + i // 2)) for i in range(4)],
                "L4": lambda: [(ct_ready, nth(c, g))],
                "LORA": lambda: [(lprep, g + 2)],
                "QK": lambda: [(k_ready, g + 1), (k_ready, g + 2), (q_ready, g + 1), (q_ready, g + 2)],
                "V": lambda: [(v_ready, g + 1)],
                "SC": lambda: [(scored, 2 * g + 1), (scored, 2 * g + 2)],
                "PV": lambda: [(oT_ready, g + 1)],
                "OUT": lambda: [(added, g + 1)],
                "AX": lambda: [(ax_ready, g // 2 + 1)],
                "Y": lambda: [(y_ready, g + 1)],
            }[kind]()

        released = [r for step in order for r in readers(step)]
        assert len(released) == n

        block = ctx.enter_context(nc.Block())

        @block.sync
        def _(sp):
            def input_free(c, g):
                before = nth(c, g) - 3
                if before >= 0:
                    pair = before % G - before % 2
                    sp.wait_ge(acc_ready, first_use[("L1", before // G, pair)] + 2)

            def first_input(g):
                input_free(0, g)
                sp.dma_start(xp[:, g % 2, :, 1:1 + M], xph[g]).then_inc(xp_in[g % 2], 16)

            def second_input(g):
                sp.wait_ge(xs_out[g % 2], 16 * (g // 2 + 1))
                input_free(1, g)
                for p in range(PH):
                    sp.dma_start(xp[32 * p:32 * p + 32, g % 2, :, 1:1 + M],
                                 scratch[g, :, p, :].rearrange("(b c) m -> c b m", b=GB)).then_inc(xp_in[g % 2], 16)

            sp.dma_start(chs[:, :], chain_s[0]).then_inc(chs_in[0], 16)
            first_input(0)
            first_input(1)
            sp.dma_start(const[:, :], consts).then_inc(const_in, 16)
            sp.dma_start(gsm[:, :, :], gates).then_inc(gate_in, 16)
            sp.wait_ge(style_ready, 1)
            sp.dma_start(chs[:, :], chain_s[1]).then_inc(chs_in[1], 16)
            first_input(2)
            first_input(3)
            sp.dma_start(bqk[:, :], bqk_d).then_inc(wide_in, 16)
            sp.dma_start(bv_row, b_qkv[2 * L:3 * L].partition_broadcast(128)).then_inc(wide_in, 16)
            sp.dma_start(bo_row, b_out.partition_broadcast(128)).then_inc(wide_in, 16)
            first_input(4)
            first_input(5)
            for g in range(G):
                sp.dma_start(xres[:, g, :], x[GB * g:GB * g + GB].rearrange("b c l -> (b c) l")).then_inc(x_in[g], 16)
            sp.dma_start(woT[:, :, :], w_outT).then_inc(wo_in, 16)
            first_input(6)
            first_input(7)
            for g in range(G):
                sp.wait_ge(xs_ready, g + 1)
                sp.dma_start(scratch[g], xs[:, g % 2]).then_inc(xs_out[g % 2], 16)
                if g == 2:
                    sp.wait_ge(ct_ready, G)
                    sp.dma_start(chw[:, :], chain_w[1]).then_inc(chw_in[1], 16)
                if g >= 1:
                    second_input(g - 1)
                if g == 5:
                    sp.wait_ge(acc_ready, first_use[("V", 0, G - 1)] + 1)
                    sp.dma_start(kff[:, :, :], ffn_w.rearrange("(m s) o -> m s o", s=PH)).then_inc(kff_in, 16)
                    sp.dma_start(aT[:, :, G, :], lora_asT).then_inc(lora_in, 16)
                    for i in range(4):
                        half = slice(64 * (i % 2) + 32, 64 * (i % 2) + 64)
                        sp.dma_start(bT[half, i // 2, :], lora_bsT).then_inc(lora_in, 16)
                    sp.wait_ge(v_ready, G)
                    sp.dma_start(bf_row, ffn_b.partition_broadcast(128)).then_inc(bf_in, 16)
                    sp.wait_ge(acc_ready, first_use[("SC", 0, G - 1)] + 2)
                    sp.dma_start(la_nat[:, :, :], lora_a.rearrange("(t n) r l -> (n r) t l", n=4)).then_inc(lora_in, 16)
                    sp.dma_start(lbT[:, :, :], lora_bT).then_inc(lora_in, 16)
            second_input(G - 1)
            for g in range(G):
                sp.wait_ge(y_ready, g + 1)
                sp.dma_start(out[GB * g:GB * g + GB].rearrange("b c l -> (b c) l"), yout[:, g % 2, :]).then_inc(y_out[g % 2], 16)
            for i in range(2):
                sp.wait_ge(y_out[i], 16 * (G // 2))

        @block.tensor
        def _(pe):
            mm = nc.tensor.matmul

            def project_style(step, c):
                a = take(pe, step)
                pe.wait_ge(chs_in[c], 16)
                for l in range(NL):
                    last = mm(a[:, B * l:B * l + B], mwT[:, l, :], styT, start=True, stop=True)
                last.then_inc(acc_ready, 1)

            def sum_squares(step, c):
                a = take(pe, step)
                pe.wait_ge(sq_ready, c + 1)
                for l in range(NL):
                    last = mm(a[:, B * l:B * l + B], w2sum[:, l].rearrange("p a b -> p (a b)"), sq[:, l, :],
                              start=True, stop=True)
                last.then_inc(acc_ready, 1)

            def demod_rows(step, c):
                pe.wait_ge(diag_ready, c + 1)
                if c == 0:
                    pe.wait_ge(zeros, 2)
                for i in range(2):
                    a = take(pe, step, i)
                    mm(a, scale32[:, :], d4diag[:, i],
                       start=True, stop=True).then_inc(acc_ready, 1)

            def layer1(step, c, g):
                a = [take(pe, step, 0), take(pe, step, 1)]
                for i in range(2):
                    if c == 0:
                        pe.wait_ge(x_scaled, g + i + 1)
                    else:
                        pe.wait_ge(xp_in[(g + i) % 2], 16 * HG + 64 * ((g + i) // 2 + 1))
                    mm(a[i], t1[:], xp[:, (g + i) % 2, :, 1:1 + M], start=True, stop=False, skip_group_check=True)
                def before(i):
                    return mm(a[i][0:32, :], wT[96:128, 2, 0, :], xp[96:128, (g + i) % 2, :, 0:M], start=False,
                              stop=False, tile_position=(96, 0), skip_group_check=True)

                def after(i):
                    return mm(a[i][96:128, :], wT[0:32, 0, 0, :], xp[0:32, (g + i) % 2, :, 2:2 + M], start=False,
                              stop=True, tile_position=(0, 96), skip_group_check=True)

                before(0)
                after(1)
                after(0)
                before(1).then_inc(acc_ready, 2)

            def layer2(step, c, g):
                a, b = take(pe, step, 0), take(pe, step, 1)
                pe.wait_ge(z1_ready, nth(c, g))
                for i, (out_, src) in enumerate(((a, z1a[:, g % 2, :, 0:M]), (b, z1b[:, g % 2]))):
                    mm(out_, t2[:, i].rearrange("p a b -> p (a b)"), src, start=True, stop=True).then_inc(acc_ready, 1)

            def layer3(step, c, g):
                a, z = [], []
                for i in range(2):
                    a.append((take(pe, step, 2 * i), take(pe, step, 2 * i + 1)))
                    z.append((z2[:, 0, (g + i) % 2], z2[:, 1, (g + i) % 2]))
                    pe.wait_ge(z2_fixed, nth(c, g + i))
                    mm(a[i][0], t3, z[i][0][:, :, 1:1 + M], start=True, stop=False, skip_group_check=True)
                    mm(a[i][1], t3b, z[i][1][:, :, 1:1 + M], start=True, stop=False, skip_group_check=True)

                def edge_product(i, tile, src, dst, tap, shift):
                    return mm(a[i][tile][dst:dst + 32, :], wT[src:src + 32, tap, 2, :],
                              z[i][1 - tile][src:src + 32, :, shift:shift + M], start=False, stop=shift == 1,
                              tile_position=(src, dst), skip_group_check=True)

                def before_0(i):
                    return edge_product(i, 0, 64, 0, 2, 0)

                def after_7(i):
                    return edge_product(i, 1, 0, 64, 0, 2)

                def after_3(i):
                    return edge_product(i, 0, 32, 96, 0, 1)

                def before_4(i):
                    return edge_product(i, 1, 96, 32, 2, 1)

                before_0(0)
                after_7(0)
                after_3(1)
                before_4(1)
                before_0(1)
                after_7(1)
                after_3(0)
                before_4(0).then_inc(acc_ready, 4)

            def layer4(step, c, g):
                a = take(pe, step)
                for tile in range(2):
                    pe.wait_ge(halo_ready[tile], nth(c, g))
                for b in range(GB):
                    o = a[:, 128 * b:128 * b + 128]
                    for i, z in enumerate((z3[:, 0, g % 2, b, 1:1 + M], z3[:, 1, g % 2, b, 1:1 + M], halo[:, g % 2, b, :])):
                        last = mm(o, z, t4[:, i].rearrange("p a b -> p (a b)"), start=i == 0, stop=i == 2)
                last.then_inc(acc_ready, 1)

            def lora(step, i):
                a = take(pe, step)
                parts = [(t, x, y) for t in range(4) for x, y in ((0, 0), (0, 1), (1, 0))]
                if i == 0:
                    pe.wait_ge(lora_in, 16 * 7)
                    pe.wait_ge(lprep, 1)
                if i < 2:
                    if i == 0:
                        pe.wait_ge(la_split, 1)
                    for half in range(2):
                        for n, (t, x, y) in enumerate(parts):
                            lhs = la[x][:, t, :].rearrange("p (m s) -> p s m", s=PH)[:, 2 * i + half, :]
                            last = mm(a[:, 256 * half:256 * half + 256], lhs, gm[y][:, t].rearrange("p g r -> p (g r)"),
                                      start=n == 0, stop=n == len(parts) - 1)
                else:
                    if i == 2:
                        pe.wait_ge(lb_split, 1)
                    h = i - 2
                    for n, (t, x, y) in enumerate(parts):
                        last = mm(a, gm[y][:, t, 4 * h:4 * h + 4, :].rearrange("p g r -> p (g r)"), lb[x][:, t, :],
                                  start=n == 0, stop=n == len(parts) - 1)
                last.then_inc(acc_ready, 1)

            def split_products(out, moving, stationary, last=True):
                high, low = 0, 1
                n = 0
                for s in range(PH):
                    for x, y in ((high, high), (high, low), (low, high)):
                        product = mm(out, stationary[x][:, s], moving[y][:, s], start=n == 0,
                                  stop=last and n == 3 * PH - 1, skip_group_check=not last)
                        n += 1
                return product

            def keys_queries(step, g):
                if g == 0:
                    pe.wait_ge(w_split, 2)
                    pe.wait_ge(w_low, 2)
                pe.wait_ge(c_split, g + 2)
                at = g % HG
                tokens = [z[:, at:at + 2].rearrange("p g s n -> p s g n") for z in (cH, cL)]
                for i in range(4):
                    a = take(pe, step, i)
                    for t in range(2):
                        col = (NT * (1 - i // 2) + 2 * (i % 2) + t) * 128
                        last = split_products(a[:, 256 * t:256 * t + 256], tokens,
                                              (wH[:, :, col:col + 128], wL[:, :, col:col + 128]))
                    last.then_inc(acc_ready, 1)

            def values_of_tokens(step, g):
                a = take(pe, step)
                split_products(a, (wH[:, :, 2 * L:3 * L], wL[:, :, 2 * L:3 * L]),
                               (cH[:, g % HG], cL[:, g % HG])).then_inc(acc_ready, 1)

            def scores(step, g):
                a = [take(pe, step, 0), take(pe, step, 1)]
                pe.wait_ge(q_ready, g - g % 2 + 2)
                for t in range(NT):
                    pe.wait_ge(km_ready[t], g + 1)
                    for b in range(GB):
                        last = mm(a[t // 2][32 * b:32 * b + 32, 256 * (t % 2):256 * (t % 2) + 256],
                                  qT[:, t, g % 2, 32 * b:32 * b + 32], km[:, t, :, 32 * b:32 * b + 32],
                                  start=True, stop=True, tile_position=(0, 32 * b))
                    if t % 2:
                        last.then_inc(acc_ready, 1)

            def values(step, g):
                a = take(pe, step)
                for r2 in range(2):
                    pe.wait_ge(pblk_ready, 2 * g + r2 + 1)
                    for t in (2 * r2, 2 * r2 + 1):
                        for e in range(2):
                            for j in range(4):
                                col = (8 * t + 2 * j) * HD
                                last = mm(a[32 * j:32 * j + 32, 128 * t:128 * t + 128], v2[:, g % 2, e, col:col + 32],
                                          pblk[:, r2, 8 * (t % 2) + 2 * j + e, :], start=e == 0, stop=e == 1,
                                          tile_position=(0, 32 * j))
                    if r2 == 0:
                        last.then_inc(pv_half, 1)
                last.then_inc(acc_ready, 1)

            def output(step, g):
                a = take(pe, step)
                if g == 0:
                    pe.wait_ge(wo_in, 16)
                pe.wait_ge(oT_ready, g + 1)
                for t in range(NT):
                    last = mm(a, oT[:, g % 2, 128 * t:128 * t + 128], woT[:, t, :], start=t == 0, stop=t == NT - 1)
                last.then_inc(acc_ready, 1)

            def low_rank(step, g):
                a = take(pe, step)
                if g == 0:
                    pe.wait_ge(lprep, 5)
                pe.wait_ge(ct_ready, nth(1, g + 1))
                for s in range(PH):
                    for i, (gi, tokens) in enumerate(((g, g), (G, g), (g + 1, g + 1), (G, g + 1))):
                        last = mm(a[32 * i:32 * i + 32, 0:128], aT[:, s, gi, :], cT[:, tokens % HG, s, :], start=s == 0, stop=s == 3,
                                  tile_position=(0, 32 * i))
                last.then_inc(acc_ready, 1)

            def feed_forward(step, g):
                a = take(pe, step)
                if g == 0:
                    pe.wait_ge(k_split, 1)
                pe.wait_ge(c2_split, g + 1)
                parts = [z[:, g % 2].rearrange("p (s n) -> p s n", s=PH) for z in (c2H, c2L)]
                split_products(a, (kH, kL), parts, last=False)
                pe.wait_ge(bt_ready, g // 2 + 1)
                pe.wait_ge(ax_ready, g // 2 + 1)
                half, slot = slice(64 * (g % 2), 64 * (g % 2) + 64), g // 2 % 2
                mm(a, axT[half, slot, :], bT[half, slot, :], start=False, stop=True, tile_position=(64 * (g % 2), 0),
                   skip_group_check=True).then_inc(acc_ready, 1)

            for step in order:
                kind, c, g = step
                if kind == "PA":
                    project_style(step, c)
                elif kind == "PB":
                    sum_squares(step, c)
                elif kind == "PC":
                    demod_rows(step, c)
                elif kind == "L1":
                    if g == 0:
                        pe.wait_ge(chw_in[c], 16)
                        pe.wait_ge(zeros, 1)
                    layer1(step, c, g)
                elif kind == "L2":
                    if g == 0:
                        pe.wait_ge(t2_ready, c + 1)
                    layer2(step, c, g)
                elif kind == "L3":
                    layer3(step, c, g)
                elif kind == "L4":
                    if g == 0:
                        pe.wait_ge(t4_ready, c + 1)
                    layer4(step, c, g)
                elif kind == "LORA":
                    lora(step, g)
                elif kind == "QK":
                    keys_queries(step, g)
                elif kind == "V":
                    values_of_tokens(step, g)
                elif kind == "SC":
                    scores(step, g)
                elif kind == "PV":
                    values(step, g)
                elif kind == "OUT":
                    output(step, g)
                elif kind == "AX":
                    low_rank(step, g)
                else:
                    feed_forward(step, g)

        @block.scalar
        def _(act):
            def scaled(dst, step, i, c, g, layer, pad=1):
                a = filled(act, step, i)
                for b in range(GB):
                    at = GB * g + b
                    last = nc.scalar.activation(dst[:, b, pad:pad + M], a[:, M * b:M * b + M], ACT.Identity,
                                                bias=tabB[:, layer, at:at + 1], scale=tabA[:, layer, at:at + 1])
                return last

            def exponentials(g):
                act.wait_ge(shifted, g + 1)
                nc.scalar.activation(S[:, g % 2, :], S[:, g % 2, :], ACT.Exp).then_inc(exp_done, 1)

            def input_to_z1(step, c, g):
                for i in range(2):
                    z1_free(act, c, g + i)
                    a, b, n_ = z1a[:, (g + i) % 2], z1b[:, (g + i) % 2], nth(c, g + i)
                    scaled(b, step, i, c, g + i, 0, pad=0).then_inc(z1b_done, 1)
                    if copied_by_act(c, g + i):
                        act.wait_ge(z1b_done, n_)
                        nc.scalar.activation(a[96:128, :, 1:M], b[96:128, :, 0:M - 1], ACT.Copy)
                        nc.scalar.activation(a[0:96, :, 0:M], b[0:96], ACT.Copy).then_inc(z1a_done, 1)
                        act.wait_ge(z1a_done, acts_copies(c, g + i))
                        nc.scalar.activation(b[0:32], a[0:32, :, 1:1 + M], ACT.Copy).then_inc(z1_ready, 1)

            nc.scalar.dma_start(chw[:, :], chain_w[0]).then_inc(chw_in[0], 16)
            for n, step in enumerate(order):
                kind, c, g = step
                if kind == "PB":
                    act.wait_ge(var_read, c + 1)
                    nc.scalar.activation(dv[:, 1].rearrange("p a b -> p (a b)"), dv[:, 0].rearrange("p a b -> p (a b)"),
                                         ACT.Sqrt).then_inc(sqrt_ready, 1)
                    if c == 0:
                        nc.scalar.dma_start(wqkvT[:, :, :], w_qkvT).then_inc(wqkv_in, 16)
                elif kind == "L1":
                    if g == 0:
                        act.wait_ge(tab_ready, c + 1)
                    input_to_z1(step, c, g)
                elif kind == "L2":
                    for i in range(1 if by_dve(c, g) else 2):
                        scaled(z2[:, i, g % 2], step, i, c, g, 1).then_inc(z2_ready[i], 1)
                    if (c, g) == (0, 3):
                        act.wait_ge(wqkv_in, 16)
                        for s in (2, 3):
                            nc.scalar.activation(wH[:, s, :], wqkvT[:, s, :], ACT.Copy).then_inc(w_high, 1)
                elif kind == "L3":
                    for g2 in (g, g + 1):
                        for tile in range(1 if by_dve(c, g) else 2):
                            z = z3[:, tile, g2 % 2]
                            scaled(z, step, 2 * (g2 - g) + tile, c, g2, 2).then_inc(z3_ready[tile], 1)
                            act.wait_ge(z3_ready[tile], nth(c, g2))
                            halo_free(act, c, g2)
                            rows_ = slice(64 * tile, 64 * tile + 64)
                            at = 0 if tile else 2
                            nc.scalar.activation(halo[rows_, g2 % 2], z[rows_, :, at:at + M],
                                                 ACT.Copy).then_inc(halo_ready[tile], 1)
                elif kind == "QK":
                    if g == 0:
                        act.wait_ge(wide_in, 48)
                    for i in range(2):
                        a = filled(act, step, 2 + i)
                        for t in (2 * i, 2 * i + 1):
                            last = nc.scalar.activation(qT[:, t].rearrange("p g n -> p (g n)"), a[:, 256 * (t % 2):256 * (t % 2) + 256],
                                                        ACT.Identity, bias=bqk[:, t:t + 1])
                        last.then_inc(q_ready, 1)
                elif kind == "PV":
                    a = filled(act, step)
                    nc.scalar.activation(oT[:, g % 2, :], a, ACT.Copy).then_inc(oT_ready, 1)
                    if g == 6:
                        act.wait_ge(lora_in, 16 * 7)
                        nc.scalar.activation(la[0][:, :, :], la_nat[:, :, :], ACT.Copy).then_inc(la_high, 1)
                    elif g == 7:
                        nc.scalar.activation(lb[0][:, :, :], lbT[:, :, :], ACT.Copy).then_inc(lb_high, 1)
                elif kind == "AX":
                    slot = g // 2 % 2
                    if g >= HG:
                        act.wait_ge(acc_ready, first_use[("Y", 1, g - 3)] + 1)
                    if g == 0:
                        act.wait_ge(lprep, 5)
                    for i in range(2):
                        q = 32 * ((g + i) % HG)
                        last = nc.scalar.activation(bT[64 * i:64 * i + 32, slot, :], bT4[q:q + 32, g // HG, :], ACT.Copy)
                    last.then_inc(bt_ready, 1)
                    a = filled(act, step)
                    nc.scalar.activation(axT[:, slot, :], a[:, 0:128], ACT.Copy).then_inc(ax_ready, 1)
                if n in exp_after:
                    exponentials(exp_after[n])

        @block.gpsimd
        def _(pool):
            tt = nc.gpsimd.tensor_tensor
            steps = [0]

            def after(ins):
                steps[0] += 1
                ins.then_inc(pool_done, 1)
                pool.wait_ge(pool_done, steps[0])

            def masked_keys(g):
                mask = const[:, C_MASK:C_MASK + 8].unsqueeze(2).broadcast_to((128, 8, 128))
                if g >= 1:
                    pool.wait_ge(acc_ready, first_use[("SC", 0, g - 1)] + 2)
                for t in range(NT):
                    pool.wait_ge(k_ready, g - g % 2 + t // 2 + 1)
                    tt(km[:, t], kT[:, t, g % 2, :].unsqueeze(1).broadcast_to((128, 8, 128)), mask,
                       ALU.mult).then_inc(km_ready[t], 1)
                    pool.wait_ge(km_ready[t], g + 1)

            after(nc.gpsimd.memset(z1a[96:128, :, :, 0], 0.0))
            after(nc.gpsimd.memset(z1a[0:32, :, :, M], 0.0))
            for pad in (0, MP - 1):
                nc.gpsimd.memset(xp[:, :, :, pad], 0.0)
            for pad in (0, MP - 1):
                for z in (z2, z3):
                    for i in range(2):
                        last = nc.gpsimd.memset(z[:, i, :, :, pad], 0.0)
            last.then_inc(zeros, 1)
            pool.wait_ge(zeros, 1)
            nc.gpsimd.memset(t2[:, :, :, :], 0.0)
            nc.gpsimd.memset(t4[:, :, :, :], 0.0)
            nc.gpsimd.memset(scale32[:, :], SCALE).then_inc(zeros, 1)
            pool.wait_ge(zeros, 2)
            nc.gpsimd.memset(pblk[:, :, :, :].rearrange("p a b c -> p (a b c)"), 0.0).then_inc(cleared, 1)
            pool.wait_ge(cleared, 1)
            for step in order:
                kind, c, g = step
                if kind == "PB":
                    pool.wait_ge(taps_ready, 2 * c + 1)
                    for row, (pa, pb) in enumerate(((0, 4), (1, 1), (2, 2), (-1, 3))):
                        q = slice(32 * row, 32 * row + 32)
                        lo, hi = max(0, 2 * pa - 2), min(PH, 2 * pa + 4)
                        after(nc.gpsimd.tensor_copy(t2[q, 0, lo:hi, :], taps2[q, lo - 2 * pa + 2:hi - 2 * pa + 2, :]))
                        lo, hi = max(PH, 2 * pb - 2), min(2 * PH, 2 * pb + 4)
                        for odd in range(2):
                            at = lo + 1 - odd - 2 * pb + 2
                            tile = nc.gpsimd.tensor_copy(t2[q, 1, lo - PH + odd:hi - PH:2, :],
                                                         taps2[q, at:at + hi - lo - 1:2, :])
                            if (row, odd) < (PH - 1, 1):
                                after(tile)
                    tile.then_inc(t2_ready, 1)
                    pool.wait_ge(t2_ready, c + 1)
                elif kind == "L2":
                    pool.wait_ge(z2_ready[0], nth(c, g))
                    pool.wait_ge(z2_ready[1], nth(c, g))
                    at = slice(GB * g, GB * g + GB)
                    first, last = z2[0:32, 0, g % 2, :, 1], z2[64:96, 1, g % 2, :, M]
                    after(tt(first, first, edge[0:32, at], ALU.subtract))
                    tt(last, last, edge[64:96, at], ALU.subtract).then_inc(z2_fixed, 1)
                    pool.wait_ge(z2_fixed, nth(c, g))
                    if g == 1:
                        pool.wait_ge(taps_ready, 2 * c + 2)
                        for p in range(PH):
                            q = slice(32 * p, 32 * p + 32)
                            for i, n in enumerate((p, TILE_B[p], p + 8 if p < 2 else TILE_B[p] - 8)):
                                ss = [s for s in range(PH) if 0 <= 3 - n + 2 * s <= 5]
                                r0 = 3 - n + 2 * ss[0]
                                tile = nc.gpsimd.tensor_copy(t4[q, i, ss[0]:ss[-1] + 1, :],
                                                             taps4[q, r0:r0 + 2 * len(ss) - 1:2, :])
                                if (p, i) < (PH - 1, 2):
                                    after(tile)
                        tile.then_inc(t4_ready, 1)
                        pool.wait_ge(t4_ready, c + 1)
                    if (c, g) == (0, 3):
                        for s in (2, 3):
                            pool.wait_ge(w_high, s - 1)
                            tt(wL[:, s, :], wqkvT[:, s, :], wH[:, s, :].bitcast(F32), ALU.subtract).then_inc(w_low, 1)
                            pool.wait_ge(w_low, s - 1)
                        nc.gpsimd.memset(v2[:, :, :, :].rearrange("p a b c -> p (a b c)"), 0.0).then_inc(cleared, 1)
                        pool.wait_ge(cleared, 2)
                elif step == ("PV", 0, 6):
                    pool.wait_ge(la_high, 1)
                    tt(la[1][:, :, :], la_nat[:, :, :], la[0][:, :, :].bitcast(F32), ALU.subtract).then_inc(la_split, 1)
                    pool.wait_ge(la_split, 1)
                elif step == ("PV", 0, 7):
                    pool.wait_ge(lb_high, 1)
                    tt(lb[1][:, :, :], lbT[:, :, :], lb[0][:, :, :].bitcast(F32), ALU.subtract).then_inc(lb_split, 1)
                    pool.wait_ge(lb_split, 1)
                elif kind == "QK":
                    masked_keys(g)
                elif kind == "SC" and g % 2 == 0:
                    masked_keys(g + 1)
                elif kind == "V":
                    if g == 0:
                        pool.wait_ge(wide_in, 48)
                    pool.wait_ge(x_in[g], 16)
                    tt(xres[:, g, :], xres[:, g, :], bo_row, ALU.add).then_inc(x_biased, 1)
                    pool.wait_ge(x_biased, g + 1)
                elif kind == "AX":
                    if g == 0:
                        pool.wait_ge(bf_in, 16)
                    for g in (g, g + 1):
                        pool.wait_ge(xs_ready, g + 1)
                        tt(xres[:, g, :], xres[:, g, :], bf_row, ALU.add).then_inc(xf_ready, 1)
                        pool.wait_ge(xf_ready, g + 1)

        @block.vector
        def _(dve):
            v = nc.vector
            tt, stt, ts, copy = v.tensor_tensor, v.scalar_tensor_tensor, v.tensor_scalar, v.tensor_copy
            links = [0]

            def link(ins):
                links[0] += 1
                ins.then_inc(dve_done, 1)
                dve.wait_ge(dve_done, links[0])

            def scale_first(g):
                dve.wait_ge(xp_in[g % 2], 16 * (g // 2 + 1))
                part = xp[:, g % 2, :, 1:1 + M]
                tt(part, part, stab2[:, 0, 0, GB * g:GB * g + GB].unsqueeze(2).broadcast_to((128, GB, M)), ALU.mult).then_inc(x_scaled, 1)

            def scale_second(g):
                if g >= 2:
                    dve.wait_ge(xs_out[g % 2], 16 * (g // 2))
                ts(xs[:, g % 2], xres[:, g, :].rearrange("p (m s) -> p s m", s=PH), sin[:, g:g + 1], None,
                   ALU.mult).then_inc(xs_ready, 1)

            def style_scales(step, c):
                if c == 0:
                    square_sums(c)
                a = filled(dve, step)
                tt(stab2[:, c], a[:, 0:NL * B].rearrange("p (l b) -> p l b", l=NL),
                   mbr.unsqueeze(2).broadcast_to((128, NL, B)), ALU.add).then_inc(style_ready, 1)
                dve.wait_ge(style_ready, c + 1)
                if c == 0:
                    tt(sq[:, :, :], stab2[0:32, 0], stab2[0:32, 0], ALU.mult).then_inc(sq_ready, 1)
                    scale_first(0)
                else:
                    for j in range(GB):
                        last = copy(sin[32 * j:32 * j + 32, :], stab2[32 * j:32 * j + 32, 1, 0, :].rearrange("p (g j) -> p j g", j=GB)[:, j, :])
                    link(last)

            def square_sums(c):
                dve.wait_ge(chw_in[c], 16)
                taps = wT[0:32].rearrange("p k l o -> p k (l o)")
                link(tt(w2sq, taps, taps, ALU.mult))
                link(v.tensor_reduce(w2one, w2sq.rearrange("p k n -> p n k"), AX_X, ALU.add))
                copy(w2sum[:, :, :, :], w2one.rearrange("p (l o) -> p l o", l=NL).unsqueeze(2).broadcast_to((32, NL, PH, C)))

            def tables(step, c):
                stab = stab2[:, c]
                link(v.memset(taps2[:, :, :], 0.0))
                for j in range(4):
                    dst = taps2[:, 3 - j:6 - j, :]
                    tap = stt(dst, w_up[:], 2.0 * BLUR[j], dst, ALU.mult, ALU.add)
                    if j < 3:
                        link(tap)
                tap.then_inc(taps_ready, 1)
                a = filled(dve, step)
                flat = [dv[:, i].rearrange("p a b -> p (a b)") for i in range(3)]
                ts(flat[0], a[:, 0:NL * B], SCALE * SCALE, EPS, ALU.mult, ALU.add).then_inc(var_read, 1)
                dve.wait_ge(var_read, c + 1)
                d = dd[:, :, :].rearrange("p a b -> p (a b)")
                if c == 0:
                    scale_first(1)
                dve.wait_ge(sqrt_ready, c + 1)
                link(v.reciprocal(flat[1], flat[1]))
                link(tt(flat[2], flat[1], flat[1], ALU.mult))
                link(tt(flat[2], flat[2], flat[0], ALU.mult))
                link(ts(flat[2], flat[2], -0.5, 1.5, ALU.mult, ALU.add))
                link(tt(d, flat[1], flat[2], ALU.mult))
                b = [cbr[:, l:l + 1] for l in range(NL)]
                stt(tabA[:, 0, :], dd[:, 0, :], SCALE, dd[:, 1, :], ALU.mult, ALU.mult)
                ts(tabB[:, 0, :], dd[:, 1, :], b[0], None, ALU.mult)
                stt(tabA[:, 1, :], stab[:, 1, :], SCALE, stab[:, 2, :], ALU.mult, ALU.mult)
                ts(tabB[:, 1, :], stab[:, 2, :], b[1], 2.0, ALU.mult, ALU.mult)
                ts(edge[:, :], stab[:, 2, :], b[1], 2.0 * BLUR_EDGE, ALU.mult, ALU.mult)
                stt(tabA[:, 2, :], dd[:, 2, :], SCALE, stab[:, 3, :], ALU.mult, ALU.mult)
                ts(tabB[:, 2, :], stab[:, 3, :], b[2], None, ALU.mult).then_inc(tab_ready, 1)
                if c == 0:
                    dve.wait_ge(const_in, 16)
                for i in range(2):
                    last = tt(d4diag[:, i].rearrange("p j (b o) -> p j b o", o=C),
                              dd[0:32, 3, 16 * i:16 * i + 16].rearrange("p (j b) -> p j b", b=4).unsqueeze(3).broadcast_to((32, 4, 4, C)),
                              const[0:32, C_SEL:C_SEL + C].unsqueeze(1).unsqueeze(1).broadcast_to((32, 4, 4, C)), ALU.mult)
                last.then_inc(diag_ready, 1)

            def last_taps():
                link(v.memset(taps4[:, :, :], 0.0))
                for j in range(4):
                    dst = taps4[:, 3 - j:6 - j, :]
                    tap = stt(dst, wT[:, :, 3, :], BLUR[j], dst, ALU.mult, ALU.add)
                    if j < 3:
                        link(tap)
                tap.then_inc(taps_ready, 1)

            def scale_rows(step, c):
                for i in range(2):
                    a = filled(dve, step, i)
                    last = copy(d4row[:, 16 * i:16 * i + 16, :].rearrange("p b o -> p (b o)"), a)
                last.then_inc(d4_ready, 1)

            def lora_gates():
                dve.wait_ge(gate_in, 16)
                sel = const[:, C_SEL:C_SEL + C].unsqueeze(1).broadcast_to((128, G, RANK))
                for t in range(4):
                    last = tt(gmat[:, t], gsm[:, t, :].unsqueeze(2).broadcast_to((128, G, RANK)), sel, ALU.mult)
                link(last)
                flat = [z[:, :, :, :].rearrange("p t g r -> p (t g r)") for z in (*gm, gmat)]
                split(*flat).then_inc(lprep, 1)

            def lora(step, i):
                a = filled(dve, step)
                if i < 2:
                    copy(aT[:, 2 * i:2 * i + 2, 0:G, :], a.rearrange("p (s g r) -> p s g r", s=2, g=G)).then_inc(lprep, 1)
                else:
                    copy(bT4[:, i - 2, :], a).then_inc(lprep, 1)

            def shifted_phases(c, g):
                for g in (g, g + 1):
                    a, b = z1a[:, g % 2], z1b[:, g % 2]
                    dve.wait_ge(z1b_done, nth(c, g))
                    copy(a[96:128, :, 1:M], b[96:128, :, 0:M - 1])
                    link(copy(a[0:96, :, 0:M], b[0:96]))
                    copy(b[0:32], a[0:32, :, 1:1 + M]).then_inc(z1_ready, 1)

            def scaled_tile_b(z, ready, step, i, c, g, layer):
                a = filled(dve, step, i)
                for b in range(GB):
                    at = GB * g + b
                    last = ts(z[:, 1, g % 2, b, 1:1 + M], a[:, M * b:M * b + M], tabA[:, layer, at:at + 1],
                              tabB[:, layer, at:at + 1], ALU.mult, ALU.add)
                last.then_inc(ready, 1)

            def down_out(step, c, g):
                a = filled(dve, step)
                view = cT[:, g % HG].rearrange("p s (b o) -> p b s o", b=GB)
                for b in range(GB):
                    last = tt(view[:, b], a[:, 128 * b:128 * b + 128].rearrange("p (s o) -> p s o", s=PH),
                              d4row[:, GB * g + b, :].unsqueeze(1).broadcast_to((128, PH, C)), ALU.mult)
                link(last)
                flat = cT[:, g % HG].rearrange("p s (b o) -> p (s b) o", b=GB)
                whole = tt(flat, flat, b4row[:, :].unsqueeze(1).broadcast_to((128, PH * GB, C)), ALU.add)
                whole.then_inc(ct_ready, 1)
                if c == 0:
                    dve.wait_ge(ct_ready, g + 1)
                    split(cH[:, g % HG], cL[:, g % HG], cT[:, g % HG]).then_inc(c_split, 1)

            def split(high, low, whole):
                link(copy(high, whole))
                return tt(low, whole, high.bitcast(F32), ALU.subtract)

            def split_weights(s):
                if s == 0:
                    dve.wait_ge(wqkv_in, 16)
                split(wH[:, s, :], wL[:, s, :], wqkvT[:, s, :]).then_inc(w_split, 1)

            def split_second(g):
                if g >= 2:
                    dve.wait_ge(acc_ready, first_use[("Y", 1, g - 2)] + 1)
                dve.wait_ge(ct_ready, nth(1, g))
                split(c2H[:, g % 2], c2L[:, g % 2], cT[:, g % HG].rearrange("p s n -> p (s n)")).then_inc(c2_split, 1)

            def keys(step, g):
                if g == 0:
                    dve.wait_ge(wide_in, 48)
                for i in range(2):
                    a = filled(dve, step, i)
                    bias = bqk[:, NT + 2 * i:NT + 2 * i + 2]
                    tt(kT[:, 2 * i:2 * i + 2].rearrange("p t g n -> p t (g n)"), a.rearrange("p (t n) -> p t n", t=2),
                       bias.unsqueeze(2).broadcast_to((128, 2, 256)), ALU.add).then_inc(k_ready, 1)

            def values_of_tokens(step, g):
                if g == 0:
                    dve.wait_ge(cleared, 2)
                a = filled(dve, step)
                for e in range(2):
                    pick = lambda ap: ap.rearrange("p (n e d) -> p e n d", e=2, d=HD)[:, e]
                    last = tt(pick(v2[:, g % 2, e, :]), pick(a), pick(bv_row), ALU.add)
                last.then_inc(v_ready, 1)

            def scores(step, g):
                for i in range(2):
                    a = filled(dve, step, i)
                    half = slice(512 * i, 512 * i + 512)
                    stt(S[:, g % 2, half], a, QK_SCALE, const[:, C_ALIBI + 512 * i:C_ALIBI + 512 * i + 512], ALU.mult,
                        ALU.add).then_inc(scored, 1)
                dve.wait_ge(scored, 2 * g + 2)
                rows_ = S[:, g % 2, :].rearrange("p (h k) -> p h k", k=C)
                link(v.tensor_reduce(stat[:, 0, g % 2, :], rows_, AX_X, ALU.max))
                tt(rows_, rows_, stat[:, 0, g % 2, :].unsqueeze(2).broadcast_to((128, HEADS, C)), ALU.subtract).then_inc(shifted, 1)

            def normalise(g):
                dve.wait_ge(exp_done, g + 1)
                rows_ = S[:, g % 2, :].rearrange("p (h k) -> p h k", k=C)
                link(v.tensor_reduce(stat[:, 1, g % 2, :], rows_, AX_X, ALU.add))
                link(v.reciprocal(stat[:, 1, g % 2, :], stat[:, 1, g % 2, :]))
                link(tt(rows_, rows_, stat[:, 1, g % 2, :].unsqueeze(2).broadcast_to((128, HEADS, C)), ALU.mult))

            def turn(g):
                for r2 in range(2):
                    if g >= 1:
                        if r2 == 0:
                            dve.wait_ge(pv_half, g)
                        else:
                            dve.wait_ge(acc_ready, first_use[("PV", 0, g - 1)] + 1)
                    for b in range(GB):
                        q = slice(32 * b, 32 * b + 32)
                        last = v.transpose(pblk[q, r2, :, 32 * b:32 * b + 32],
                                           S[q, g % 2, 512 * r2:512 * r2 + 512].rearrange("p (h k) -> p h k", k=C))
                    last.then_inc(pblk_ready, 1)

            def residual(step, g):
                a = filled(dve, step)
                dve.wait_ge(x_biased, g + 1)
                tt(xres[:, g, :], xres[:, g, :], a, ALU.add).then_inc(added, 1)
                dve.wait_ge(added, g + 1)
                scale_second(g)

            def last_sum(step, g):
                a = filled(dve, step)
                dve.wait_ge(xf_ready, g + 1)
                if g >= 2:
                    dve.wait_ge(y_out[g % 2], 16 * (g // 2))
                else:
                    dve.wait_ge(xs_out[g], 16 * (G // 2))
                tt(yout[:, g % 2, :], a, xres[:, g, :], ALU.add).then_inc(y_ready, 1)

            weights_after = {order.index(step): s for s, step in enumerate(of(0, "L1.2 L2.3"))}
            split_after = {max(order.index(("L4", 1, g)), order.index(("Y", 1, g - 2)) if g >= 2 else 0): g for g in range(G)}
            assert len(split_after) == G
            scale_after = {order.index(step): g for g, step in zip(range(2, G), of(0, "PC.0 L2.0 L2.2 L2.3 L2.4 L2.5"))}
            for n, step in enumerate(order):
                kind, c, g = step
                if kind == "PA":
                    style_scales(step, c)
                elif kind == "PB":
                    tables(step, c)
                elif kind == "PC":
                    scale_rows(step, c)
                elif kind == "LORA":
                    lora(step, g)
                    if g == 1:
                        dve.wait_ge(kff_in, 16)
                        split(kH[:, :, :], kL[:, :, :], kff[:, :, :]).then_inc(k_split, 1)
                elif kind == "L1":
                    if not copied_by_act(c, g):
                        shifted_phases(c, g)
                    if (c, g) == (1, 0):
                        last_taps()
                elif kind == "L2" and by_dve(c, g):
                    if g % HG == 0:
                        dve.wait_ge(tab_ready, c + 1)
                    scaled_tile_b(z2, z2_ready[1], step, 1, c, g, 1)
                    if (c, g) == (0, 1):
                        last_taps()
                    if (c, g) == (1, 3):
                        lora_gates()
                elif kind == "L3" and by_dve(c, g):
                    for i in range(2):
                        scaled_tile_b(z3, z3_ready[1], step, 2 * i + 1, c, g + i, 2)
                        dve.wait_ge(z3_ready[1], nth(c, g + i))
                        halo_free(dve, c, g + i)
                        copy(halo[64:128, (g + i) % 2], z3[64:128, 1, (g + i) % 2, :, 0:M]).then_inc(halo_ready[1], 1)
                elif kind == "L4":
                    down_out(step, c, g)
                elif kind == "QK":
                    keys(step, g)
                elif kind == "V":
                    values_of_tokens(step, g)
                elif kind == "SC":
                    scores(step, g)
                elif kind == "OUT":
                    residual(step, g)
                    if g == HG - 1:
                        square_sums(1)
                        tt(sq[:, :, :], stab2[0:32, 1], stab2[0:32, 1], ALU.mult).then_inc(sq_ready, 1)
                elif kind == "Y":
                    last_sum(step, g)
                if n in split_after:
                    split_second(split_after[n])
                if n in norm_after:
                    normalise(norm_after[n])
                if n in turn_after:
                    turn(turn_after[n])
                if n in scale_after:
                    scale_first(scale_after[n])
                if n in weights_after:
                    split_weights(weights_after[n])


_INS = ["x", "cond_512"] + [f"L0_{c}_{n}" for c in ("cond", "cond2") for n in ("weights", "biases", "mod_w", "mod_b")] + [
    "L0_attn_w_qkv", "L0_attn_b_qkv", "L0_attn_w_out", "L0_attn_b_out", "L0_ffn_gate", "L0_ffn_kernel", "L0_ffn_bias",
    "L0_ffn_lora_A", "L0_ffn_lora_B", "L0_ffn_lora_A_shared", "L0_ffn_lora_B_shared"]


def kernel(**inputs):
    import concourse.bacc as bacc
    from concourse.bass_utils import run_bass_kernel_spmd

    nc = bacc.Bacc("TRN2", target_bir_lowering=False, num_devices=1)
    v = {n: np.ascontiguousarray(inputs[n]) for n in _INS}
    attn, ffn = "L0_attn_", "L0_ffn_"
    arrays = {
        "x": v["x"],
        "xph": v["x"].reshape(G, GB, C, M, PH).transpose(0, 4, 2, 1, 3).reshape(G, 128, GB, M),
        "w_qkvT": v[attn + "w_qkv"].T.reshape(M, PH, NQKV * 128),
        "bqk": v[attn + "b_qkv"][:2 * L].reshape(2 * NT, 128).T,
        "b_qkv": v[attn + "b_qkv"],
        "w_outT": v[attn + "w_out"].T.reshape(NT, 128, L).transpose(1, 0, 2),
        "b_out": v[attn + "b_out"],
        "gates": np.repeat(v[ffn + "gate"].T.reshape(4, 4, G).transpose(1, 0, 2), RANK, axis=0),
        "ffn_w": v[ffn + "kernel"],
        "ffn_b": v[ffn + "bias"],
        "lora_a": v[ffn + "lora_A"],
        "lora_bT": v[ffn + "lora_B"].transpose(0, 2, 1).reshape(4, 4 * RANK, L).transpose(1, 0, 2),
        "lora_asT": v[ffn + "lora_A_shared"].T.reshape(M, PH, RANK),
        "lora_bsT": v[ffn + "lora_B_shared"].T,
        "consts": shape_constants(),
    }
    for i, c in enumerate(("cond", "cond2")):
        arrays[f"chain_w{i}"], arrays[f"chain_s{i}"] = pack_chain(
            *(v[f"L0_{c}_{n}"] for n in ("weights", "biases", "mod_w", "mod_b")), v["cond_512"])
    arrays = {n: np.ascontiguousarray(a) for n, a in arrays.items()}
    d = {n: nc.dram_tensor("in_" + n, a.shape, mybir.dt.from_np(a.dtype), kind="ExternalInput").ap() for n, a in arrays.items()}
    out = nc.dram_tensor("out", (B, C, L), F32, kind="ExternalOutput").ap()
    build(nc, d["x"], d["xph"], [d["chain_w0"], d["chain_w1"]], [d["chain_s0"], d["chain_s1"]], d["w_qkvT"], d["bqk"],
          d["b_qkv"], d["w_outT"], d["b_out"], d["gates"], d["ffn_w"], d["ffn_b"], d["lora_a"], d["lora_bT"],
          d["lora_asT"], d["lora_bsT"], d["consts"], out)
    arrays = {"in_" + n: a for n, a in arrays.items()}
    r = run_bass_kernel_spmd(nc, [arrays], core_ids=[0])
    return r.results[0]["out"]
```
